# Optimizing a Trainium2 kernel written in Bass

```python
import numpy as np
import jax
import jax.numpy as jnp

def _softmax(x, axis=-1):
    return jax.nn.softmax(x, axis=axis)

def _gelu(x):
    return jax.nn.gelu(x, approximate=True)

def _silu(x):
    return jax.nn.silu(x)

def _sigmoid(x):
    return jax.nn.sigmoid(x)

def _layernorm(x, axis=-1, eps=1e-05):
    m = jnp.mean(x, axis=axis, keepdims=True)
    v = jnp.var(x, axis=axis, keepdims=True)
    return (x - m) / jnp.sqrt(v + eps)

def _scatter_add(tgt, idx, src, axis=0):
    return tgt.at[idx].add(src)

def _segment_sum(src, seg, n):
    return jax.ops.segment_sum(src, seg, n)
kernel_name = 'mk_decoder_postln_d1_seqx_r4_f511cb'

def setup_inputs(seed: int=0):
    np.random.seed(seed)
    _w = jnp.asarray

    def _rec_inputs():
        import jax
        import jax.numpy as jnp
        _rk = jax.random.key(seed)
        x = -0.0002928 + 1 * jax.random.normal(jax.random.fold_in(_rk, 1), (16, 256, 256), jnp.float32)
        _lenS = 256 - jax.random.randint(jax.random.fold_in(_rk, 7), (16,), 0, max(1, 256 // 4) + 1, jnp.int32)
        _lenS2 = 256 - jax.random.randint(jax.random.fold_in(_rk, 8), (16,), 0, max(1, 256 // 4) + 1, jnp.int32)
        _ctx_1024P = jax.random.normal(jax.random.fold_in(_rk, 11), (16, 16, 256), jnp.float32)
        _ctx_1024c = jax.random.dirichlet(jax.random.fold_in(_rk, 511), 0.3 * jnp.ones((16,), jnp.float32), (16, 256))
        _ctx_1024t = jnp.einsum('bsk,bkd->bsd', _ctx_1024c, _ctx_1024P)
        _ctx_1024t = _ctx_1024t * jax.lax.rsqrt(jnp.mean(jnp.square(_ctx_1024t)) + 1e-12) * 0.953939
        ctx_1024 = -1.39393e-06 + 0.999914 * (_ctx_1024t + 0.3 * jax.random.normal(jax.random.fold_in(_rk, 611), (16, 256, 256), jnp.float32))
        return (x, ctx_1024)
    x, ctx_1024 = _rec_inputs()

    def _L0_attn_setup():
        import jax, jax.numpy as jnp
        import numpy as np
        N_HEADS = 16
        D_MODEL = 256
        SEQ_LEN = 512
        BATCH = 4
        key = jax.random.key(seed)
        k1, k2, k3 = jax.random.split(key, 3)
        std = 1.0 / np.sqrt(D_MODEL)
        x = jax.random.normal(k1, (BATCH, SEQ_LEN, D_MODEL), dtype=jnp.float32)
        w_qkv = std * jax.random.normal(k2, (D_MODEL, 3 * D_MODEL), dtype=jnp.float32)
        w_o = std * jax.random.normal(k3, (D_MODEL, D_MODEL), dtype=jnp.float32)
        return {'x': x, 'w_qkv': w_qkv, 'w_o': w_o}
    _L0_attn_all = _L0_attn_setup()
    _L0_attn_in = {k: v for k, v in _L0_attn_all.items() if k in ('w_qkv', 'w_o')}
    del _L0_attn_all

    def _L0_xattn_setup():
        import jax, jax.numpy as jnp
        import numpy as np
        DIM = 256
        NUM_HEADS = 16
        HEAD_DIM = DIM // NUM_HEADS
        key = jax.random.key(seed)
        ks = jax.random.split(key, 11)
        B, N, C = (2, 512, DIM)
        s = 1.0 / np.sqrt(C)
        inp = {'q': jax.random.normal(ks[0], (B, N, C), jnp.float32), 'k': jax.random.normal(ks[1], (B, N, C), jnp.float32), 'v': jax.random.normal(ks[2], (B, N, C), jnp.float32), 'Wq': jax.random.normal(ks[3], (C, C), jnp.float32) * s, 'bq': jnp.zeros((C,), jnp.float32), 'Wk': jax.random.normal(ks[4], (C, C), jnp.float32) * s, 'bk': jnp.zeros((C,), jnp.float32), 'Wv': jax.random.normal(ks[5], (C, C), jnp.float32) * s, 'bv': jnp.zeros((C,), jnp.float32), 'Wo': jax.random.normal(ks[6], (C, C), jnp.float32) * s, 'bo': jnp.zeros((C,), jnp.float32)}
        return inp
    _L0_xattn_all = _L0_xattn_setup()
    _L0_xattn_in = {k: v for k, v in _L0_xattn_all.items() if k in ('Wq', 'bq', 'Wk', 'bk', 'Wv', 'bv', 'Wo', 'bo')}
    del _L0_xattn_all

    def _L0_ffn_setup():
        import jax, jax.numpy as jnp
        import numpy as np
        DIM = 256
        HIDDEN = 768
        SCALE = 1.0 / 127.0

        def _dequant(w_int, dtype):
            return w_int.astype(dtype) * jnp.asarray(SCALE, dtype)
        key = jax.random.key(seed)
        k_x, k_g, k_u, k_d = jax.random.split(key, 4)
        x = jax.random.normal(k_x, (4, 512, DIM), dtype=jnp.float32)
        w_gate = jax.random.randint(k_g, (HIDDEN, DIM), -127, 128, dtype=jnp.int32)
        w_up = jax.random.randint(k_u, (HIDDEN, DIM), -127, 128, dtype=jnp.int32)
        w_down = jax.random.randint(k_d, (DIM, HIDDEN), -127, 128, dtype=jnp.int32)
        return {'x': x, 'w_gate': w_gate, 'w_up': w_up, 'w_down': w_down}
    _L0_ffn_all = _L0_ffn_setup()
    _L0_ffn_in = {k: v for k, v in _L0_ffn_all.items() if k in ('w_gate', 'w_up', 'w_down')}
    del _L0_ffn_all
    return {'x': x, 'ctx_1024': ctx_1024, 'L0_attn_w_qkv': _L0_attn_in['w_qkv'], 'L0_attn_w_o': _L0_attn_in['w_o'], 'L0_xattn_Wq': _L0_xattn_in['Wq'], 'L0_xattn_bq': _L0_xattn_in['bq'], 'L0_xattn_Wk': _L0_xattn_in['Wk'], 'L0_xattn_bk': _L0_xattn_in['bk'], 'L0_xattn_Wv': _L0_xattn_in['Wv'], 'L0_xattn_bv': _L0_xattn_in['bv'], 'L0_xattn_Wo': _L0_xattn_in['Wo'], 'L0_xattn_bo': _L0_xattn_in['bo'], 'L0_ffn_w_gate': _L0_ffn_in['w_gate'], 'L0_ffn_w_up': _L0_ffn_in['w_up'], 'L0_ffn_w_down': _L0_ffn_in['w_down']}

def reference(x, ctx_1024, L0_attn_w_qkv, L0_attn_w_o, L0_xattn_Wq, L0_xattn_bq, L0_xattn_Wk, L0_xattn_bk, L0_xattn_Wv, L0_xattn_bv, L0_xattn_Wo, L0_xattn_bo, L0_ffn_w_gate, L0_ffn_w_up, L0_ffn_w_down):
    import jax
    import jax.numpy as jnp

    def _L0_attn_ref(x, w_qkv, w_o):
        import jax, jax.numpy as jnp
        import numpy as np
        N_HEADS = 16
        D_MODEL = 256
        SEQ_LEN = 512
        BATCH = 4
        *lead, seq_len, d_model = x.shape
        head_dim = d_model // N_HEADS
        qkv = x @ w_qkv
        qkv = qkv.reshape(*qkv.shape[:-1], N_HEADS, 3 * head_dim)
        qkv = jnp.einsum('...Thd->...hTd', qkv)
        q, k, v = jnp.split(qkv, 3, axis=-1)
        scores = jnp.einsum('...hqd,...hkd->...hqk', q, k) / np.sqrt(d_model).astype(x.dtype)
        causal = jnp.tri(seq_len, dtype=bool)
        scores = jnp.where(causal, scores, jnp.asarray(-1e+30, dtype=scores.dtype))
        attn = jax.nn.softmax(scores, axis=-1)
        out = jnp.einsum('...hqk,...hkd->...qhd', attn, v)
        out = out.reshape(*out.shape[:-2], d_model)
        return out @ w_o

    def _L0_xattn_ref(q, k, v, Wq, bq, Wk, bk, Wv, bv, Wo, bo):
        import jax, jax.numpy as jnp
        import numpy as np
        DIM = 256
        NUM_HEADS = 16
        HEAD_DIM = DIM // NUM_HEADS
        B, Nq, C = q.shape
        Nkv = k.shape[1]
        H, D = (NUM_HEADS, HEAD_DIM)
        qh = (q @ Wq.T + bq).reshape(B, Nq, H, D).transpose(0, 2, 1, 3)
        kh = (k @ Wk.T + bk).reshape(B, Nkv, H, D).transpose(0, 2, 1, 3)
        vh = (v @ Wv.T + bv).reshape(B, Nkv, H, D).transpose(0, 2, 1, 3)
        scale = D ** (-0.5)
        attn = jax.nn.softmax(jnp.einsum('bhqd,bhkd->bhqk', qh, kh) * scale, axis=-1)
        out = jnp.einsum('bhqk,bhkd->bhqd', attn, vh)
        out = out.transpose(0, 2, 1, 3).reshape(B, Nq, C)
        return out @ Wo.T + bo

    def _L0_ffn_ref(x, w_gate, w_up, w_down):
        import jax, jax.numpy as jnp
        import numpy as np
        DIM = 256
        HIDDEN = 768
        SCALE = 1.0 / 127.0

        def _dequant(w_int, dtype):
            return w_int.astype(dtype) * jnp.asarray(SCALE, dtype)
        wg = _dequant(w_gate, x.dtype)
        wu = _dequant(w_up, x.dtype)
        wd = _dequant(w_down, x.dtype)
        gate = jnp.einsum('bsd,hd->bsh', x, wg)
        up = jnp.einsum('bsd,hd->bsh', x, wu)
        h = jax.nn.silu(gate) * up
        return jnp.einsum('bsh,dh->bsd', h, wd)
    x = _layernorm(x + _L0_attn_ref(x, L0_attn_w_qkv, L0_attn_w_o), axis=-1)
    x = _layernorm(x + _L0_xattn_ref(x, ctx_1024, ctx_1024, L0_xattn_Wq, L0_xattn_bq, L0_xattn_Wk, L0_xattn_bk, L0_xattn_Wv, L0_xattn_bv, L0_xattn_Wo, L0_xattn_bo), axis=-1)
    x = _layernorm(x + _L0_ffn_ref(x, L0_ffn_w_gate, L0_ffn_w_up, L0_ffn_w_down), axis=-1)
    return x

_drawn_inputs = setup_inputs


def setup_inputs(seed=0):
    import zlib

    import numpy as np

    out = dict(_drawn_inputs(seed))
    spreads = {'L0_xattn_bq': (0.0, 0.277),
     'L0_xattn_bk': (0.0, 0.8),
     'L0_xattn_bv': (0.0, 0.1),
     'L0_xattn_bo': (0.0, 0.1)}
    factors = {}
    for name, (base, spread) in spreads.items():
        noise = np.random.default_rng([zlib.crc32(name.encode()), seed]).standard_normal(out[name].shape)
        drawn = base * np.exp(spread * noise) if base else spread * noise
        out[name] = jnp.asarray(drawn.astype(out[name].dtype))
    for name, factor in factors.items():
        out[name] = (out[name] * factor).astype(out[name].dtype)
    return out
```

```python
from contextlib import ExitStack

import concourse.bass as bass
from concourse import mybir

P = 128
SEQS, SEQ, D = 16, 256, 256
HEADS, HD = 16, 16
HIDDEN = 768
GROUP = 2
TOK = GROUP * SEQ
TT = TOK // P
GROUPS = SEQS // GROUP
DK = D // P
HK = HIDDEN // P
PAIRS = HEADS // 2
SLOT = P // 2
MAX_ROW = 3 * HD
VW = 32
EPS = 1e-5
MASKED = -1e30
QSCALE = 1.0 / 127.0
SELF_SCALE = 1.0 / 16.0
CROSS_SCALE = 1.0 / 4.0
WEIGHTS = ["sq", "sk", "sv", "so", "cq", "ck", "cv", "co"]
PROBS = 3
SCORE_LEAD = 22
WEIGH_LAG = 2
STAGES = {"c0": 0, "c1": 1, "s0": 2, "s1": 3}


def front_steps():
    return ([("transpose", "x", 0), ("transpose", "x", 1), ("project", "sq", 0), ("project", "sq", 1), ("value", "sv", 0)]
            + [("stack", "sq", t) for t in range(PAIRS)]
            + [("project", "sk", 0), ("project", "sk", 1), ("value", "sv", 1)]
            + [("stack", "sk", t) for t in range(PAIRS)])


def back_steps():
    return ([("transpose", "x1", 0), ("transpose", "x1", 1), ("project", "cq", 0), ("project", "cq", 1)]
            + [("transpose", "ctx", 0), ("transpose", "ctx", 1)]
            + [("stack", "cq", t) for t in range(PAIRS)]
            + [("project", "ck", 0), ("project", "ck", 1), ("value", "cv", 0)]
            + [("stack", "ck", t) for t in range(PAIRS)] + [("value", "cv", 1)])


def ffn_steps():
    steps = [("transpose", "x2", 0), ("transpose", "x2", 1)]
    for k in range(HK):
        steps += [("gate", "", k), ("up", "", k)]
    return steps + [("down", "", 0), ("down", "", 1)]


def attention_steps(stages, with_ffn):
    steps, total = [], HEADS * len(stages)
    ffn, ffn_from = (ffn_steps() if with_ffn else []), None
    for n in range(total + SCORE_LEAD + WEIGH_LAG + 6):
        if n < total:
            steps.append(("scores", stages[n // HEADS], n % HEADS))
        j = (n - HEADS - 1) // HEADS
        if n >= HEADS + 1 and (n - HEADS - 1) % HEADS == 0 and j < len(stages):
            steps.append(("maxima", stages[j], 0))
        m = n - SCORE_LEAD
        if 0 <= m < total:
            steps.append(("exps", stages[m // HEADS], m % HEADS))
        w = m - WEIGH_LAG
        if 0 <= w < total:
            steps.append(("weigh", stages[w // HEADS], w % HEADS))
        j, after = (w - (HEADS - 1)) // HEADS, (w - (HEADS - 1)) % HEADS
        if w >= HEADS - 1 and j < len(stages):
            st = stages[j]
            if after == 1:
                steps += [("normalise", st, 0), ("normalise", st, 1)]
            if after == 3:
                steps.append(("turn", st, 0))
            if after == 5:
                steps.append(("output", st, 0))
                if st == "c1":
                    ffn_from = n + 4
        if ffn_from is not None and n >= ffn_from:
            steps += ffn[:1]
            ffn = ffn[1:]
    return steps + ffn


PROLOGUE = front_steps() + attention_steps(["s0", "s1"], False)
BODY = front_steps() + back_steps() + attention_steps(["c0", "c1", "s0", "s1"], True)
EPILOGUE = back_steps() + attention_steps(["c0", "c1"], True)


def drained_by(step):
    kind, what, n = step
    if kind == "stack":
        return "act" if n % 2 == 0 else "dve"
    return "act" if (kind, what) == ("value", "sv") else "dve"


def signals(step):
    kind, what, n = step
    out = {}
    if kind not in ("scores", "exps", "weigh"):
        out["made"] = 1
        out["drained_" + drained_by(step)] = 1
    if kind in ("transpose", "project", "turn", "gate"):
        out["high"] = 1
    if kind == "scores":
        out["scores"] = out["row_max"] = 1
    if kind == "maxima":
        out["max_sent"] = 32
        out["neg_max"] = 2 if what[0] == "s" else 0
    if kind == "exps":
        out["logits"] = out["exps"] = 1
        out["masked"] = 1 if what[0] == "s" else 0
    if kind == "weigh" and n % 8 == 7:
        out["summed"] = out["unweighed"] = 1
    if kind == "normalise":
        out["dve_own"] = 1
    if kind in ("output", "down"):
        out["dve_own"], out["stats"], out["pool_own"] = 1, 2, 2
        out["x1" if what[:1] == "s" else "x2" if what[:1] == "c" else "y"] = 2
    if kind == "up":
        out["hidden"] = 1
        out["pool_own"] = 1
    if kind == "down":
        out["stored"] = 16
    if (kind, n) == ("transpose", 0) and what in ("x", "x1"):
        out["residual_" + what] = 1
    if (kind, n) == ("transpose", 0) and what in ("x", "ctx"):
        out["loaded_" + what] = 16
    return out


NAMES = sorted({name for table in (BODY, EPILOGUE) for step in table for name in signals(step)})


class Tally:

    def __init__(self):
        self.start = {name: 0 for name in NAMES}
        self.local = dict(self.start)
        self.marks = {}

    def enter(self, turn):
        for name in NAMES:
            total = {t: sum(signals(s).get(name, 0) for s in t_steps) for t, t_steps in (("p", PROLOGUE), ("b", BODY))}
            self.start[name] = turn * total["b"] + total["p"]
            self.local[name] = 0

    def now(self, name):
        return self.start[name] + self.local[name]

    def passed(self, step):
        for name, n in signals(step).items():
            self.local[name] += n
            self.marks[step, name] = self.now(name)

    def after(self, step, name):
        return self.marks[step, name]

    def slot(self, name):
        return self.local[name] % 2


def wait_for(eng, sem, value):
    if not (isinstance(value, int) and value <= 0):
        eng.wait_ge(sem, value)


def decoder_layer(nc, x, ctx_in, weights, w_gate_up, w_down, bias_qk, bias_vo, selectors, ident_in, mask_in, out):
    f32, f32r, bf16, i32 = mybir.dt.float32, mybir.dt.float32r, mybir.dt.bfloat16, mybir.dt.int32
    ALU, ACT, AX = mybir.AluOpType, mybir.ActivationFunctionType, mybir.AxisListType.X

    stack = ExitStack()
    with stack:
        def sb(name, shape, dt=f32):
            return stack.enter_context(nc.sbuf_tensor(name, shape, dt))

        w_hi = sb("w_hi", [P, len(WEIGHTS), DK, D], f32r)
        w_lo = sb("w_lo", [P, len(WEIGHTS), DK, D], f32r)
        gate_up = sb("gate_up", [P, 2, DK, HIDDEN], f32r)
        down_w = sb("down_w", [P, HK, D], f32r)
        select = sb("select", [P, 4, 4, P], f32r)
        ident = sb("ident", [P, P])
        ident_bf = sb("ident_bf", [P, P], bf16)
        causal = sb("causal", [P, P], bf16)
        b_qk = sb("b_qk", [P, 5])
        b_vo = sb("b_vo", [P, 2, D])
        half = sb("half", [P, 2])
        x_in = sb("x_in", [P, TT, D])
        ctx = sb("ctx", [P, TT, D])
        r1 = sb("r1", [P, TT, D])
        x1 = sb("x1", [P, TT, D])
        r2 = sb("r2", [P, TT, D])
        t_hi = sb("t_hi", [P, DK, TOK], f32r)
        t_lo = sb("t_lo", [P, DK, TOK], f32r)
        p_hi = sb("p_hi", [P, DK, TOK], f32r)
        p_lo = sb("p_lo", [P, DK, TOK], f32r)
        stacks = {w: sb("stack_" + w, [P, PAIRS, TOK], f32r) for w in ("sq", "sk", "cq", "ck")}
        h_hi, h_lo = stacks["cq"], stacks["ck"]
        values = {w: sb("values_" + w, [P, TT, HEADS, VW]) for w in ("sv", "cv")}
        row_max = sb("row_max", [P, 2, 3, HEADS])
        neg_max = sb("neg_max", [P, 2, 2, HEADS])
        max_t = sb("max_t", [HEADS, SEQ], f32r)
        probs = sb("probs", [P, PROBS, 2 * SEQ])
        o_un = sb("o_un", [P, 4, SEQ])
        inv = sb("inv", [P, 2, HEADS])
        o_tok = sb("o_tok", [P, 2, D])
        o_hi = sb("o_hi", [P, DK, SEQ], f32r)
        o_lo = sb("o_lo", [P, DK, SEQ], f32r)
        tanh = sb("tanh", [P, 2, TOK])
        gated = sb("gated", [P, TOK])
        hidden = sb("hidden", [P, 2, TOK])
        bn = sb("bn", [P, 2, 6])
        norms = {w: sb("norm_" + w, [P, TT, 2]) for w in ("x1", "x2", "y")}
        ve = sb("ve", [P, 2])
        rstd = sb("rstd", [P, 2])

        general = stack.enter_context(nc.psum_tensor("general", [P, 2, 512], f32))
        score = stack.enter_context(nc.psum_tensor("score", [P, 2, 512], f32))
        logit = stack.enter_context(nc.psum_tensor("logit", [P, 2, 512], f32))
        summed = stack.enter_context(nc.psum_tensor("summed", [P, 2, 512], f32))

        sem = {name: stack.enter_context(nc.semaphore(name)) for name in NAMES}
        consts_in = stack.enter_context(nc.semaphore("consts_in"))
        staged = [stack.enter_context(nc.semaphore(f"staged{n}")) for n in range(6)]
        unstaged = stack.enter_context(nc.semaphore("unstaged"))
        prepared = stack.enter_context(nc.semaphore("prepared"))
        waited = stack.enter_context(nc.semaphore("waited"))
        lot_hi = stack.enter_context(nc.semaphore("lot_hi"))
        block = stack.enter_context(nc.Block())

        def group_rows(dram, g):
            return dram.rearrange("(g t p) d -> g p t d", t=TT, p=P)[g]

        def feature_bias(what, j):
            return {"cq": b_qk[:, j:j + 1], "ck": b_qk[:, 2 + j:3 + j]}.get(what, 0.0)

        def head_index(h):
            return (h % 2) * PAIRS + h // 2

        def apart(eng):
            eng.sem_inc(waited, 1)

        def tables(eng, tally, walk):
            walk(PROLOGUE, 0, None)
            with eng.Fori(0, GROUPS - 1) as i:
                tally.enter(i)
                walk(BODY, i + 1, i)
            tally.enter(GROUPS - 1)
            walk(EPILOGUE, None, GROUPS - 1)

        stage = [values["sv"][:].rearrange("p a b c -> p (a b c)"), values["cv"][:].rearrange("p a b c -> p (a b c)")]
        LOTS = [(weights[:, 0:2048], 2048, f32), (weights[:, 2048:4096], 2048, f32), (w_gate_up[:, 0:1536], 1536, i32),
                (w_gate_up[:, 1536:3072], 1536, i32), (w_down, 1536, i32), (selectors, 2048, f32)]

        @block.sync
        def _(sp):
            for dst, src in ((ident, ident_in), (probs[:, 0, 0:P], mask_in), (b_qk, bias_qk), (b_vo, bias_vo)):
                sp.dma_start(dst[:], src).then_inc(consts_in, 16)
            for n, (src, cols, dt) in enumerate(LOTS):
                if n >= 2:
                    sp.wait_ge(unstaged, n - 1)
                sp.dma_start(stage[n % 2][:, 0:cols].bitcast(dt), src).then_inc(staged[n], 16)
            tally = Tally()
            sp.sem_inc(sem["stored"], 1)
            sp.dma_start(x_in[:], group_rows(x, 0)).then_inc(sem["loaded_x"], 16)
            sp.dma_start(ctx[:], group_rows(ctx_in, 0)).then_inc(sem["loaded_ctx"], 16)

            def walk(steps, front, back):
                for step in steps:
                    kind, what, n = step
                    if (kind, what, n) == ("transpose", "x", 1):
                        sp.wait_ge(sem["made"], tally.now("made") + 1)
                        apart(sp)
                        sp.wait_ge(sem["residual_x"], tally.now("residual_x"))
                        apart(sp)
                        sp.dma_start(x_in[:], group_rows(x, (front + 1) % GROUPS)).then_inc(sem["loaded_x"], 16)
                    if (kind, what, n) == ("transpose", "ctx", 1) and steps is BODY:
                        sp.wait_ge(sem["made"], tally.now("made") + 1)
                        apart(sp)
                        sp.dma_start(ctx[:], group_rows(ctx_in, back + 1)).then_inc(sem["loaded_ctx"], 16)
                    if kind == "maxima":
                        b = int(what[1])
                        q = stacks[what[0] + "q"]
                        sp.wait_ge(sem["drained_dve"], tally.now("drained_dve") + 1)
                        for s in range(2):
                            row = s * SLOT + MAX_ROW
                            sp.dma_start(q[row:row + 1, :, b * SEQ:(b + 1) * SEQ].bitcast(f32),
                                         max_t[s * PAIRS:(s + 1) * PAIRS, :].bitcast(f32)).then_inc(sem["max_sent"], 16)
                    if kind == "down":
                        sp.wait_ge(sem["y"], tally.now("y") + 2)
                        apart(sp)
                        rows = group_rows(out, back)
                        sp.dma_start(rows[:, 2 * n:2 * n + 2, :], r2[:, 2 * n:2 * n + 2, :]).then_inc(sem["stored"], 16)
                    tally.passed(step)
            tables(sp, tally, walk)
            sp.wait_ge(sem["loaded_x"], tally.now("loaded_x") + 16)
            sp.wait_ge(sem["stored"], tally.now("stored") + 1)

        @block.tensor
        def _(pe):
            pe.wait_ge(consts_in, 64)
            pe.wait_ge(prepared, 1)
            tally = Tally()

            def split_matmuls(dst, lhs, rhs):
                terms = [(l, r, k) for k in range(DK) for l, r in ((lhs[0], rhs[0]), (lhs[1], rhs[0]), (lhs[0], rhs[1]))]
                for n, (l, r, k) in enumerate(terms):
                    last = nc.tensor.matmul(dst, l(k), r(k), start=(n == 0), stop=(n == len(terms) - 1))
                return last

            def walk(steps, front, back):
                drains = []
                for step in steps:
                    kind, what, n = step
                    if "made" in signals(step):
                        bank = general[:, tally.slot("made"), :]
                        if len(drains) >= 2:
                            pe.wait_ge(sem[drains[-2][0]], drains[-2][1])
                        elif steps is not PROLOGUE:
                            pe.wait_ge(sem["drained_dve"], tally.start["drained_dve"])
                            pe.wait_ge(sem["drained_act"], tally.start["drained_act"])
                        by = "drained_" + drained_by(step)
                        drains.append((by, tally.now(by) + 1))

                    if kind == "transpose":
                        src = {"x": x_in, "x1": x1, "ctx": ctx, "x2": r2}[what]
                        if what in ("x", "ctx"):
                            name = "loaded_" + what
                            pe.wait_ge(sem[name], tally.now(name) + (16 if n == 0 else 0))
                        else:
                            pe.wait_ge(sem[what], tally.now(what))
                        for tt in range(TT):
                            last = nc.tensor.transpose(bank[:, tt * P:(tt + 1) * P], src[:, tt, n * P:(n + 1) * P], ident[:])
                        last.then_inc(sem["made"], 1)

                    if kind in ("project", "value"):
                        src = {"sq": "x", "sk": "x", "sv": "x", "cq": "x1", "ck": "ctx", "cv": "ctx"}[what]
                        pe.wait_ge(sem["drained_dve"], tally.after(("transpose", src, 1), "drained_dve"))
                        w = WEIGHTS.index(what)
                        if kind == "project":
                            cols = slice(n * P, (n + 1) * P)
                            last = split_matmuls(bank,
                                                 [lambda k, w_=w_: w_[:, w, k, cols] for w_ in (w_hi, w_lo)],
                                                 [lambda k, t_=t_: t_[:, k, :] for t_ in (t_hi, t_lo)])
                        else:
                            for m in range(2):
                                tok = slice((2 * n + m) * P, (2 * n + m + 1) * P)
                                last = split_matmuls(bank[:, m * D:(m + 1) * D],
                                                     [lambda k, t_=t_: t_[:, k, tok] for t_ in (t_hi, t_lo)],
                                                     [lambda k, w_=w_: w_[:, w, k, :] for w_ in (w_hi, w_lo)])
                        last.then_inc(sem["made"], 1)

                    if kind == "stack":
                        j = n // 4
                        pe.wait_ge(sem["drained_dve"], tally.after(("project", what, j), "drained_dve"))
                        which = 0 if what[1] == "q" else 2
                        nc.tensor.matmul(bank, select[:, which, n % 4, :], p_hi[:, j, :], start=True, stop=False)
                        nc.tensor.matmul(bank, select[:, which + 1, n % 4, :], p_lo[:, j, :],
                                         start=False, stop=True).then_inc(sem["made"], 1)

                    if kind == "scores":
                        b, rows, t = int(what[1]), slice((n % 2) * SLOT, (n % 2 + 1) * SLOT), n // 2
                        q, k = stacks[what[0] + "q"], stacks[what[0] + "k"]
                        base = b * SEQ
                        if n < 2 * PAIRS:
                            for w in ("q", "k"):
                                made = ("stack", what[0] + w, t)
                                by = "drained_" + drained_by(made)
                                pe.wait_ge(sem[by], tally.after(made, by))
                        wait_for(pe, sem["row_max"], tally.now("row_max") - 1)
                        bank = score[:, tally.slot("scores"), :]
                        if what[0] == "c":
                            for qt in range(2):
                                last = nc.tensor.matmul(bank[:, qt * SEQ:(qt + 1) * SEQ], q[rows, t, base + qt * P:base + (qt + 1) * P],
                                                        k[rows, t, base:base + SEQ], start=True, stop=True)
                        else:
                            nc.tensor.matmul(bank[:, 0:P], q[rows, t, base:base + P], k[rows, t, base:base + P],
                                             start=True, stop=False, skip_group_check=True)
                            nc.tensor.matmul(bank[:, P:3 * P], q[rows, t, base + P:base + 2 * P], k[rows, t, base:base + SEQ],
                                             start=False, stop=False, skip_group_check=True)
                            diagonal = bank[:, 0:4 * P].rearrange("p (a b c) -> p a b c", a=2, b=2)[:, :, 0, :]
                            last = nc.tensor.matmul(diagonal, ident_bf[:], causal[:].unsqueeze(1).broadcast_to([P, 2, P]),
                                                    start=False, stop=True, skip_group_check=True)
                        last.then_inc(sem["scores"], 1)

                    if kind == "maxima":
                        if what[0] == "s":
                            pe.wait_ge(sem["neg_max"], tally.now("neg_max") + 2)
                        else:
                            pe.wait_ge(sem["row_max"], tally.after(("scores", what, HEADS - 1), "row_max"))
                        for qt in range(2):
                            last = nc.tensor.transpose(bank[0:HEADS, qt * P:(qt + 1) * P], neg_max[:, STAGES[what] % 2, qt, :], ident[:])
                        last.then_inc(sem["made"], 1)

                    if kind == "exps":
                        b, rows, t = int(what[1]), slice((n % 2) * SLOT, (n % 2 + 1) * SLOT), n // 2
                        q, k = stacks[what[0] + "q"], stacks[what[0] + "k"]
                        base = b * SEQ
                        if n == 0:
                            pe.wait_ge(sem["max_sent"], tally.after(("maxima", what, 0), "max_sent"))
                        wait_for(pe, sem["exps"], tally.now("exps") - 1)
                        bank = logit[:, tally.slot("logits"), :]
                        nc.tensor.matmul(bank[:, 0:SEQ], k[rows, t, base:base + P], q[rows, t, base:base + SEQ], start=True, stop=True)
                        if what[0] == "c":
                            last = nc.tensor.matmul(bank[:, SEQ:2 * SEQ], k[rows, t, base + P:base + 2 * P], q[rows, t, base:base + SEQ],
                                                    start=True, stop=True)
                        else:
                            last = nc.tensor.matmul(bank[:, SEQ:SEQ + P], k[rows, t, base + P:base + 2 * P],
                                                    q[rows, t, base + P:base + 2 * P], start=True, stop=True)
                        last.then_inc(sem["logits"], 1)

                    if kind == "weigh":
                        b, c, g = int(what[1]), n % 4, n // 4
                        v = values[what[0] + "v"]
                        if n == 0:
                            for half_ in range(2):
                                made = ("value", what[0] + "v", half_)
                                by = "drained_" + drained_by(made)
                                pe.wait_ge(sem[by], tally.after(made, by))
                        ready = "masked" if what[0] == "s" else "exps"
                        pe.wait_ge(sem[ready], tally.after(("exps", what, n), ready))
                        if n % 8 == 0:
                            wait_for(pe, sem["unweighed"], tally.now("unweighed") - 1)
                        pr = probs[:, tally_probs[what, n], :]
                        dst = summed[c * 32:(c + 1) * 32, n // 8, (g % 2) * SEQ:(g % 2 + 1) * SEQ]
                        nc.tensor.matmul(dst, v[:, 2 * b, n, :], pr[:, 0:SEQ], start=True, stop=False, skip_group_check=True)
                        if what[0] == "c":
                            last = nc.tensor.matmul(dst, v[:, 2 * b + 1, n, :], pr[:, SEQ:2 * SEQ], start=False, stop=True,
                                                    skip_group_check=True)
                        else:
                            last = nc.tensor.matmul(dst[:, P:2 * P], v[:, 2 * b + 1, n, :], pr[:, SEQ:SEQ + P], start=False, stop=True,
                                                    skip_group_check=True)
                        if n % 8 == 7:
                            last.then_inc(sem["summed"], 1)

                    if kind == "normalise":
                        pe.wait_ge(sem["unweighed"], tally.after(("weigh", what, HEADS - 1), "unweighed"))
                        for g in range(4):
                            last = nc.tensor.transpose(bank[:, g * P:(g + 1) * P], o_un[:, g, n * P:(n + 1) * P], ident[:])
                        last.then_inc(sem["made"], 1)

                    if kind == "turn":
                        pe.wait_ge(sem["drained_dve"], tally.after(("normalise", what, 1), "drained_dve"))
                        for k in range(DK):
                            for tt in range(2):
                                last = nc.tensor.transpose(bank[:, k * SEQ + tt * P:k * SEQ + (tt + 1) * P],
                                                           o_tok[:, tt, k * P:(k + 1) * P], ident[:])
                        last.then_inc(sem["made"], 1)

                    if kind == "output":
                        pe.wait_ge(sem["drained_dve"], tally.after(("turn", what, 0), "drained_dve"))
                        w = WEIGHTS.index(what[0] + "o")
                        for m in range(2):
                            tok = slice(m * P, (m + 1) * P)
                            last = split_matmuls(bank[:, m * D:(m + 1) * D],
                                                 [lambda k, t_=t_: t_[:, k, tok] for t_ in (o_hi, o_lo)],
                                                 [lambda k, w_=w_: w_[:, w, k, :] for w_ in (w_hi, w_lo)])
                        last.then_inc(sem["made"], 1)

                    if kind in ("gate", "up"):
                        pe.wait_ge(sem["drained_dve"], tally.after(("transpose", "x2", 1), "drained_dve"))
                        for k in range(DK):
                            for part in (t_hi, t_lo):
                                last = nc.tensor.matmul(bank, gate_up[:, int(kind == "up"), k, n * P:(n + 1) * P], part[:, k, :],
                                                        start=(k == 0 and part is t_hi), stop=(k == DK - 1 and part is t_lo))
                        last.then_inc(sem["made"], 1)

                    if kind == "down":
                        pe.wait_ge(sem["hidden"], tally.after(("up", "", HK - 1), "hidden"))
                        for m in range(2):
                            tok = slice((2 * n + m) * P, (2 * n + m + 1) * P)
                            for k in range(HK):
                                for part in (h_hi, h_lo):
                                    last = nc.tensor.matmul(bank[:, m * D:(m + 1) * D], part[:, k, tok], down_w[:, k, :],
                                                            start=(k == 0 and part is h_hi), stop=(k == HK - 1 and part is h_lo))
                        last.then_inc(sem["made"], 1)
                    if kind == "exps":
                        tally_probs[what, n] = tally.local["exps"] % PROBS
                    tally.passed(step)
            tally_probs = {}
            tables(pe, tally, walk)

        @block.scalar
        def _(act):
            act.wait_ge(consts_in, 64)
            act.wait_ge(prepared, 1)
            tally = Tally()

            def walk(steps, front, back):
                for step in steps:
                    kind, what, n = step
                    bank = general[:, tally.slot("made"), :]
                    if kind in ("transpose", "project", "turn"):
                        act.wait_ge(sem["made"], tally.now("made") + 1)
                        if kind == "turn":
                            nc.scalar.activation(o_hi[:].rearrange("p k t -> p (k t)"), bank, ACT.Identity).then_inc(sem["high"], 1)
                        elif kind == "transpose":
                            nc.scalar.activation(t_hi[:, n, :], bank, ACT.Identity).then_inc(sem["high"], 1)
                        else:
                            nc.scalar.activation(p_hi[:, n, :], bank, ACT.Identity,
                                                 bias=feature_bias(what, n)).then_inc(sem["high"], 1)
                    if kind == "stack" and drained_by(step) == "act":
                        act.wait_ge(sem["made"], tally.now("made") + 1)
                        nc.scalar.activation(stacks[what][:, n, :], bank, ACT.Identity,
                                             bias=b_qk[:, 4:5] if what[1] == "k" else 0.0).then_inc(sem["drained_act"], 1)
                    if (kind, what) == ("value", "sv"):
                        act.wait_ge(sem["made"], tally.now("made") + 1)
                        nc.scalar.copy(values["sv"][:, 2 * n:2 * n + 2, :, 0:HD],
                                       bank.rearrange("p (t h d) -> p t h d", t=2, h=HEADS)).then_inc(sem["drained_act"], 1)
                    if kind == "exps":
                        width = 2 * SEQ if what[0] == "c" else SEQ + P
                        act.wait_ge(sem["logits"], tally.now("logits") + 1)
                        nc.scalar.activation(probs[:, tally.local["exps"] % PROBS, 0:width], logit[:, tally.slot("logits"), 0:width], ACT.Exp,
                                             scale=CROSS_SCALE if what[0] == "c" else SELF_SCALE).then_inc(sem["exps"], 1)
                    if kind == "weigh" and n % 8 == 7:
                        act.wait_ge(sem["summed"], tally.now("summed") + 1)
                        nc.scalar.copy(o_un[:, 2 * (n // 8):2 * (n // 8) + 2, :],
                                       summed[:, n // 8, :].rearrange("p (g q) -> p g q", g=2)).then_inc(sem["unweighed"], 1)
                    if kind == "gate":
                        act.wait_ge(sem["made"], tally.now("made") + 1)
                        nc.scalar.activation(tanh[:, n % 2, :], bank, ACT.Tanh, scale=0.5 * QSCALE).then_inc(sem["high"], 1)
                    tally.passed(step)
            tables(act, tally, walk)

        @block.vector
        def _(dve):
            dve.wait_ge(consts_in, 64)
            nc.vector.tensor_copy(ident_bf[:], ident[:])
            nc.vector.tensor_copy(causal[:], probs[:, 0, 0:P])
            nc.vector.memset(half[:], -0.5)
            w_hi2, w_lo2 = (w[:].rearrange("p a b c -> p (a b c)") for w in (w_hi, w_lo))
            gate_up2 = gate_up[:].rearrange("p a b c -> p (a b c)")
            for n, (_, cols, dt) in enumerate(LOTS):
                dve.wait_ge(staged[n], 16)
                src = stage[n % 2][:, 0:cols].bitcast(dt)
                if n < 2:
                    part = slice(n * cols, (n + 1) * cols)
                    nc.vector.tensor_copy(w_hi2[:, part], src).then_inc(lot_hi, 1)
                    dve.wait_ge(lot_hi, n + 1)
                    nc.vector.tensor_tensor(w_lo2[:, part], src, w_hi2[:, part].bitcast(f32), ALU.subtract).then_inc(unstaged, 1)
                else:
                    dst = [gate_up2[:, 0:1536], gate_up2[:, 1536:3072], down_w[:].rearrange("p k d -> p (k d)"),
                           select[:].rearrange("p a b c -> p (a b c)")][n - 2]
                    nc.vector.tensor_copy(dst, src).then_inc(unstaged, 1)
            dve.wait_ge(unstaged, len(LOTS))
            for n, w in enumerate(("sv", "cv")):
                nc.vector.memset(values[w][:, :, :, HD + 1:VW], 0.0)
                last = nc.vector.memset(values[w][:, :, :, HD:HD + 1], 1.0)
            last.then_inc(prepared, 1)
            tally = Tally()

            def own(ins):
                own_done[0] += 1
                ins.then_inc(sem["dve_own"], 1)
                dve.wait_ge(sem["dve_own"], tally.now("dve_own") + own_done[0])
            own_done = [0]

            def normalise_stats(rows, which, first):
                for m in range(2):
                    last = nc.vector.bn_stats(bn[:, m, :], rows[:, first + m, :])
                    if m == 1:
                        own(last)
                        apart(dve)
                for m in range(2):
                    last = nc.vector.bn_aggr(norms[which][:, first + m, :], bn[:, m, :])
                    last.then_inc(sem["stats"], 1)

            def walk(steps, front, back):
                for step in steps:
                    kind, what, n = step
                    own_done[0] = 0
                    bank = general[:, tally.slot("made"), :]
                    mine = "drained_dve" in signals(step)
                    if mine and kind != "maxima":
                        dve.wait_ge(sem["made"], tally.now("made") + 1)
                    if kind in ("transpose", "project", "turn"):
                        dve.wait_ge(sem["high"], tally.now("high") + 1)
                        if kind == "turn":
                            nc.vector.tensor_tensor(o_lo[:].rearrange("p k t -> p (k t)"), bank,
                                                    o_hi[:].rearrange("p k t -> p (k t)").bitcast(f32), ALU.subtract).then_inc(sem["drained_dve"], 1)
                        elif kind == "transpose":
                            nc.vector.tensor_tensor(t_lo[:, n, :], bank, t_hi[:, n, :].bitcast(f32), ALU.subtract).then_inc(sem["drained_dve"], 1)
                        else:
                            nc.vector.scalar_tensor_tensor(out=p_lo[:, n, :], in0=bank, scalar=feature_bias(what, n),
                                                           in1=p_hi[:, n, :].bitcast(f32), op0=ALU.add,
                                                           op1=ALU.subtract).then_inc(sem["drained_dve"], 1)
                    if kind == "stack" and mine:
                        if what[1] == "k":
                            ins = nc.vector.tensor_scalar(stacks[what][:, n, :], bank, b_qk[:, 4:5], None, ALU.add)
                        else:
                            ins = nc.vector.tensor_copy(stacks[what][:, n, :], bank)
                        ins.then_inc(sem["drained_dve"], 1)
                    if (kind, what) == ("value", "cv"):
                        nc.vector.tensor_tensor(values["cv"][:, 2 * n:2 * n + 2, :, 0:HD],
                                                bank.rearrange("p (t h d) -> p t h d", t=2, h=HEADS),
                                                b_vo[:, 0, :].rearrange("p (h d) -> p h d", h=HEADS).unsqueeze(1).broadcast_to([P, 2, HEADS, HD]),
                                                ALU.add).then_inc(sem["drained_dve"], 1)
                    if kind == "scores":
                        dve.wait_ge(sem["scores"], tally.now("scores") + 1)
                        bank, at, par = score[:, tally.slot("scores"), :], head_index(n), STAGES[what] % 2
                        if what[0] == "c":
                            nc.vector.tensor_reduce(neg_max[:, par, :, at], bank.rearrange("p (t k) -> p t k", t=2), AX, ALU.max,
                                                    negate=True).then_inc(sem["row_max"], 1)
                        else:
                            nc.vector.tensor_reduce(row_max[:, par, :, at], bank[:, 0:3 * P].rearrange("p (t k) -> p t k", t=3), AX,
                                                    ALU.max, negate=True).then_inc(sem["row_max"], 1)
                    if kind == "maxima":
                        par = STAGES[what] % 2
                        if what[0] == "s":
                            dve.wait_ge(sem["row_max"], tally.after(("scores", what, HEADS - 1), "row_max"))
                            nc.vector.tensor_copy(neg_max[:, par, 0, :], row_max[:, par, 0, :]).then_inc(sem["neg_max"], 1)
                            nc.vector.tensor_tensor(neg_max[:, par, 1, :], row_max[:, par, 1, :], row_max[:, par, 2, :],
                                                    ALU.min).then_inc(sem["neg_max"], 1)
                        dve.wait_ge(sem["made"], tally.now("made") + 1)
                        wait_for(dve, sem["max_sent"], tally.now("max_sent"))
                        nc.vector.tensor_copy(max_t[:], bank[0:HEADS, 0:SEQ]).then_inc(sem["drained_dve"], 1)
                    if kind == "normalise":
                        heads = bank.rearrange("p (h c) -> p h c", c=VW)
                        own(nc.vector.reciprocal(inv[:, n, :], heads[:, :, HD]))
                        nc.vector.tensor_tensor(o_tok[:, n, :].rearrange("p (h d) -> p h d", d=HD), heads[:, :, 0:HD],
                                                inv[:, n, :].unsqueeze(2).broadcast_to([P, HEADS, HD]), ALU.mult).then_inc(sem["drained_dve"], 1)
                    if kind == "output":
                        b, which = int(what[1]), "x1" if what[0] == "s" else "x2"
                        rows = r1 if what[0] == "s" else r2
                        res = "residual_x" if what[0] == "s" else "residual_x1"
                        dve.wait_ge(sem[res], tally.now(res))
                        ins = nc.vector.tensor_tensor(rows[:, 2 * b:2 * b + 2, :], bank.rearrange("p (t d) -> p t d", t=2),
                                                      rows[:, 2 * b:2 * b + 2, :], ALU.add)
                        ins.then_inc(sem["drained_dve"], 1)
                        dve.wait_ge(sem["drained_dve"], tally.now("drained_dve") + 1)
                        normalise_stats(rows, which, 2 * b)
                    if kind == "gate":
                        if n >= 1:
                            dve.wait_ge(sem["drained_dve"], tally.after(("up", "", n - 1), "drained_dve"))
                        dve.wait_ge(sem["high"], tally.now("high") + 1)
                        nc.vector.scalar_tensor_tensor(out=gated[:], in0=tanh[:, n % 2, :], scalar=1.0, in1=bank,
                                                       op0=ALU.add, op1=ALU.mult).then_inc(sem["drained_dve"], 1)
                    if kind == "up":
                        dve.wait_ge(sem["drained_dve"], tally.after(("gate", "", n), "drained_dve"))
                        if n >= 2:
                            dve.wait_ge(sem["hidden"], tally.after(("up", "", n - 2), "hidden"))
                        nc.vector.tensor_tensor(hidden[:, n % 2, :], gated[:], bank, ALU.mult).then_inc(sem["drained_dve"], 1)
                    if kind == "down":
                        rows = r2[:, 2 * n:2 * n + 2, :]
                        nc.vector.scalar_tensor_tensor(out=rows, in0=bank.rearrange("p (t d) -> p t d", t=2), scalar=0.5 * QSCALE ** 3,
                                                       in1=rows, op0=ALU.mult, op1=ALU.add).then_inc(sem["drained_dve"], 1)
                        dve.wait_ge(sem["drained_dve"], tally.now("drained_dve") + 1)
                        normalise_stats(r2, "y", 2 * n)
                    tally.passed(step)
            tables(dve, tally, walk)

        @block.gpsimd
        def _(pool):
            pool.wait_ge(prepared, 1)
            tally = Tally()

            def own(ins):
                own_done[0] += 1
                ins.then_inc(sem["pool_own"], 1)
                pool.wait_ge(sem["pool_own"], tally.now("pool_own") + own_done[0])
                apart(pool)
            own_done = [0]

            def normalise(dst, rows, which, first):
                pool.wait_ge(sem["stats"], tally.now("stats") + 2)
                apart(pool)
                mv = norms[which]
                own(nc.gpsimd.tensor_scalar(ve[:], mv[:, first:first + 2, 1], EPS, None, ALU.add))
                own(nc.gpsimd.tensor_tensor(rstd[:], ve[:], half[:], ALU.pow))
                for m in range(2):
                    nc.gpsimd.tensor_scalar(dst[:, first + m, :], rows[:, first + m, :], mv[:, first + m, 0:1], rstd[:, m:m + 1],
                                            ALU.subtract, ALU.mult).then_inc(sem[which], 1)

            def walk(steps, front, back):
                for step in steps:
                    kind, what, n = step
                    own_done[0] = 0
                    if (kind, n) == ("transpose", 0) and what == "x":
                        pool.wait_ge(sem["loaded_x"], tally.now("loaded_x") + 16)
                        wait_for(pool, sem["x1"], tally.now("x1"))
                        apart(pool)
                        nc.gpsimd.tensor_copy(r1[:], x_in[:]).then_inc(sem["residual_x"], 1)
                    if (kind, n) == ("transpose", 0) and what == "x1":
                        pool.wait_ge(sem["x1"], tally.now("x1"))
                        pool.wait_ge(sem["stored"], tally.now("stored") + 1)
                        apart(pool)
                        nc.gpsimd.tensor_tensor(r2[:], x1[:], b_vo[:, 1, :].unsqueeze(1).broadcast_to([P, TT, D]),
                                                ALU.add).then_inc(sem["residual_x1"], 1)
                    if kind == "exps" and what[0] == "s":
                        pool.wait_ge(sem["exps"], tally.now("exps") + 1)
                        apart(pool)
                        blocks = probs[:, tally.local["exps"] % PROBS, :].rearrange("p (a b) -> p a b", a=2)[:, :, 0:P]
                        nc.gpsimd.affine_select(out=blocks, in_=blocks, compare_op=ALU.is_ge, fill=0.0, base=0,
                                                pattern=[[0, 2], [1, P]], channel_multiplier=-1).then_inc(sem["masked"], 1)
                    if kind == "output":
                        b = int(what[1])
                        normalise(*((x1, r1, "x1") if what[0] == "s" else (r2, r2, "x2")), 2 * b)
                    if kind == "up":
                        pool.wait_ge(sem["drained_dve"], tally.now("drained_dve") + 1)
                        apart(pool)
                        own(nc.gpsimd.tensor_copy(h_hi[:, n, :], hidden[:, n % 2, :]))
                        nc.gpsimd.tensor_tensor(h_lo[:, n, :], hidden[:, n % 2, :], h_hi[:, n, :].bitcast(f32),
                                                ALU.subtract).then_inc(sem["hidden"], 1)
                    if kind == "down":
                        normalise(r2, r2, "y", 2 * n)
                    tally.passed(step)
            tables(pool, tally, walk)


def _constants():
    import numpy as np
    places = {0: (0, 2), 1: (1,), 2: (0, 1), 3: (2,)}
    sel = np.zeros((P, 4, 4, P), np.float32)
    for which, blocks in places.items():
        for t in range(4):
            for s in range(2):
                for d in range(HD):
                    for blk in blocks:
                        sel[(2 * t + s) * HD + d, which, t, s * SLOT + blk * HD + d] = 1.0
    row = np.arange(P)
    mask = np.where(row[None, :] > row[:, None], MASKED, 0.0).astype(np.float32)
    one_row = (row % SLOT == MAX_ROW).astype(np.float32)[:, None]
    return sel.reshape(P, -1), np.eye(P, dtype=np.float32), mask, one_row


def kernel(**inputs):
    import numpy as np
    import concourse.bacc as _bacc
    from concourse import mybir as _mybir
    from concourse.bass_utils import run_bass_kernel_spmd as _run

    a = {name: np.asarray(v) for name, v in inputs.items()}

    def rows(w):
        return w.reshape(-1, P, w.shape[1]).transpose(1, 0, 2)

    qkv = a["L0_attn_w_qkv"].reshape(D, HEADS, 3, HD).transpose(2, 0, 1, 3).reshape(3, D, D)
    mats = [qkv[0], qkv[1], qkv[2], a["L0_attn_w_o"]] + [a["L0_xattn_W" + n].T for n in "qkvo"]
    weights = np.stack([rows(m) for m in mats], 1).reshape(P, -1)
    gate_up = np.stack([rows(a["L0_ffn_w_gate"].T), rows(a["L0_ffn_w_up"].T)], 1).reshape(P, -1)
    down = rows(a["L0_ffn_w_down"].T).reshape(P, -1)
    sel, eye, mask, one_row = _constants()
    bias_qk = np.concatenate([a["L0_xattn_bq"].reshape(2, P).T, a["L0_xattn_bk"].reshape(2, P).T, one_row], 1)
    bias_vo = np.broadcast_to(np.stack([a["L0_xattn_bv"], a["L0_xattn_bo"]])[None], (P, 2, D))
    laid = {"x": a["x"].reshape(SEQS * SEQ, D), "ctx": a["ctx_1024"].reshape(SEQS * SEQ, D), "weights": weights,
            "gate_up": gate_up, "down": down, "bias_qk": bias_qk, "bias_vo": bias_vo, "selectors": sel, "ident": eye, "mask": mask}

    nc = _bacc.Bacc("TRN2", target_bir_lowering=False, num_devices=1)
    nc.disable_value_cache = True
    arrays, args = {}, []
    for name, value in laid.items():
        value = np.ascontiguousarray(value)
        arrays[name + "_dram"] = value
        args.append(nc.dram_tensor(name + "_dram", value.shape, _mybir.dt.from_np(value.dtype), kind="ExternalInput").ap())
    y = nc.dram_tensor("y_dram", (SEQS * SEQ, D), _mybir.dt.float32, kind="ExternalOutput").ap()
    decoder_layer(nc, *args, y)
    r = _run(nc, [arrays], core_ids=[0])
    return r.results[0]["y_dram"].reshape(SEQS, SEQ, D)
```

```python
from contextlib import ExitStack

import concourse.bass as bass
from concourse import mybir

P = 128
SEQS, SEQ, D = 16, 256, 256
HEADS, HD = 16, 16
HIDDEN = 768
GROUP = 2
TOK = GROUP * SEQ
TT = TOK // P
GROUPS = SEQS // GROUP
DK = D // P
HK = HIDDEN // P
PAIRS = HEADS // 2
SLOT = P // 2
MAX_ROW = 3 * HD
VW = 32
SELECT_AT = {("q", "hi"): HD, ("k", "hi"): 0, ("q", "lo"): 4 * P + HD, ("k", "lo"): 4 * P + 3 * HD}
SELECTS = 8 * P + 3 * HD
EPS = 1e-5
MASKED = -1e30
QSCALE = 1.0 / 127.0
SELF_SCALE = 1.0 / 16.0
CROSS_SCALE = 1.0 / 4.0
WEIGHTS = ["sq", "sk", "sv", "so", "cq", "ck", "cv", "co"]
PROBS = 6
SCORE_LEAD = 22
WEIGH_LAG = 2
STAGES = {"c0": 0, "c1": 1, "s0": 2, "s1": 3}


X_SIDE = ([("transpose", "x", 0), ("transpose", "x", 1), ("project", "sq", 0), ("project", "sq", 1), ("value", "sv", 0)]
          + [("stack", "sq", t) for t in range(PAIRS)]
          + [("project", "sk", 0), ("project", "sk", 1), ("value", "sv", 1)]
          + [("stack", "sk", t) for t in range(PAIRS)])
X1_SIDE = ([("transpose", "x1", 0), ("transpose", "x1", 1), ("project", "cq", 0), ("project", "cq", 1)]
           + [("stack", "cq", t) for t in range(PAIRS)])
CTX_SIDE = [("transpose", "ctx", 0), ("transpose", "ctx", 1), ("project", "ck", 0), ("project", "ck", 1),
            ("value", "cv", 0), ("value", "cv", 1)]
CTX_STACKS = [("stack", "ck", t) for t in range(PAIRS)]
FFN = [("transpose", "x2", 0), ("transpose", "x2", 1)]
for _k in range(HK):
    FFN += [("gate", "", _k), ("up", "", _k)] + ([("split", "", _k - 1)] if _k else [])
FFN += [("split", "", HK - 1)]
DOWN = [("down", "", 0), ("down", "", 1), ("norm", "y0", 0), ("norm", "y1", 0)]
FREE = ("split", "norm")


def attention_steps(stages, early, late):
    steps, total, late_from = [], HEADS * len(stages), None
    early, late = list(early), list(late)
    if "c1" not in stages:
        late_from = HEADS + SCORE_LEAD
    for n in range(total + SCORE_LEAD + WEIGH_LAG + 8):
        if n < total:
            steps.append(("scores", stages[n // HEADS], n % HEADS))
        j = (n - HEADS - 1) // HEADS
        if n >= HEADS + 1 and (n - HEADS - 1) % HEADS == 0 and j < len(stages):
            steps.append(("maxima", stages[j], 0))
        m = n - SCORE_LEAD
        if 0 <= m < total:
            steps.append(("exps", stages[m // HEADS], m % HEADS))
        w = m - WEIGH_LAG
        if 0 <= w < total and w % 4 == 3:
            steps.append(("weigh", stages[w // HEADS], w % HEADS // 4))
        j, after = (w - (HEADS - 1)) // HEADS, (w - (HEADS - 1)) % HEADS
        if w >= HEADS - 1 and j < len(stages):
            st = stages[j]
            if after == 1:
                steps += [("normalise", st, 0), ("normalise", st, 1)]
            if after == 3:
                steps.append(("turn", st, 0))
            if after == 5:
                steps.append(("output", st, 0))
            if after == 6:
                steps.append(("norm", st, 0))
                if st == "c1":
                    late_from = n + 1
        if early:
            steps.append(early.pop(0))
        elif late and late_from is not None and n >= late_from:
            steps.append(late.pop(0))
            while late and late[0][0] in FREE:
                steps.append(late.pop(0))
    return steps + late


PROLOGUE = X_SIDE + attention_steps(["s0", "s1"], [], CTX_SIDE + CTX_STACKS)
BODY = X1_SIDE + attention_steps(["c0", "c1", "s0", "s1"], X_SIDE, FFN + DOWN + CTX_SIDE + CTX_STACKS)
EPILOGUE = X1_SIDE + attention_steps(["c0", "c1"], [], FFN + DOWN)


def drained_by(step):
    kind, what, n = step
    if kind == "stack":
        return "act" if what[0] == "s" or n % 2 == 0 else "dve"
    return "act" if (kind, what) == ("value", "sv") else "dve"


def signals(step):
    kind, what, n = step
    out = {}
    if kind not in ("scores", "exps", "weigh") + FREE:
        out["made"] = 1
        out["drained_" + drained_by(step)] = 1
    if kind in ("transpose", "project", "turn", "gate"):
        out["high"] = 1
    if kind == "scores":
        out["scores"] = out["row_max"] = 1
    if kind == "maxima":
        out["max_sent"] = 32
        out["neg_max"] = 2 if what[0] == "s" else 0
    if kind == "exps":
        out["logits"] = out["exps"] = 1
        out["masked"] = 1 if what[0] == "s" else 0
    if kind == "weigh" and n % 2 == 1:
        out["summed"] = out["unweighed"] = 1
    if kind == "normalise":
        out["dve_own"] = 1
    if kind in ("output", "down"):
        out["dve_own"], out["stats"], out["pool_own"], out["rstd"] = 1, 2, 1, 1
    if kind == "norm":
        out[{"s": "x1", "c": "x2", "y": "y"}[what[0]]] = 2
    if kind == "split":
        out["hidden_high"] = out["hidden"] = 1
    if (kind, what[:1]) == ("norm", "y"):
        out["stored"] = 16
    if (kind, n) == ("transpose", 0) and what in ("x", "x1"):
        out["residual_" + what] = 1
    if (kind, n) == ("transpose", 0) and what in ("x", "ctx"):
        out["loaded_" + what] = 16
    return out


NAMES = sorted({name for table in (BODY, EPILOGUE) for step in table for name in signals(step)})


class Tally:

    def __init__(self):
        self.start = {name: 0 for name in NAMES}
        self.local = dict(self.start)
        self.marks = {}

    def enter(self, turn):
        self.marks = {}
        for name in NAMES:
            total = {t: sum(signals(s).get(name, 0) for s in t_steps) for t, t_steps in (("p", PROLOGUE), ("b", BODY))}
            self.start[name] = turn * total["b"] + total["p"]
            self.local[name] = 0

    def now(self, name):
        return self.start[name] + self.local[name]

    def passed(self, step):
        for name, n in signals(step).items():
            self.local[name] += n
            self.marks[step, name] = self.now(name)

    def after(self, step, name):
        return self.marks.get((step, name), self.start[name])

    def slot(self, name):
        return self.local[name] % 2


def wait_for(eng, sem, value):
    if not (isinstance(value, int) and value <= 0):
        eng.wait_ge(sem, value)


def decoder_layer(nc, x, ctx_in, weights, w_gate_up, w_down, bias_qk, bias_vo, selectors, ident_in, mask_in, out):
    f32, f32r, bf16, i32 = mybir.dt.float32, mybir.dt.float32r, mybir.dt.bfloat16, mybir.dt.int32
    ALU, ACT, AX = mybir.AluOpType, mybir.ActivationFunctionType, mybir.AxisListType.X

    stack = ExitStack()
    with stack:
        def sb(name, shape, dt=f32):
            return stack.enter_context(nc.sbuf_tensor(name, shape, dt))

        w_hi = sb("w_hi", [P, len(WEIGHTS), DK, D], f32r)
        w_lo = sb("w_lo", [P, len(WEIGHTS), DK, D], f32r)
        gate_up = sb("gate_up", [P, 2, DK, HIDDEN], f32r)
        down_w = sb("down_w", [P, HK, D], f32r)
        select = sb("select", [P, SELECTS], f32r)
        ident = sb("ident", [P, P])
        ident_bf = sb("ident_bf", [P, P], bf16)
        causal = sb("causal", [P, P], bf16)
        b_qk = sb("b_qk", [P, 5])
        b_vo = sb("b_vo", [P, 2, D])
        half = sb("half", [P, 2])
        x_in = sb("x_in", [P, TT, D])
        ctx = sb("ctx", [P, TT, D])
        r1 = sb("r1", [P, TT, D])
        x1 = sb("x1", [P, TT, D])
        r2 = sb("r2", [P, TT, D])
        t_hi = sb("t_hi", [P, DK, TOK], f32r)
        t_lo = sb("t_lo", [P, DK, TOK], f32r)
        p_hi = sb("p_hi", [P, DK, TOK], f32r)
        p_lo = sb("p_lo", [P, DK, TOK], f32r)
        stacks = {w: sb("stack_" + w, [P, PAIRS, TOK], f32r) for w in ("sq", "sk", "cq", "ck")}
        h_hi, h_lo = stacks["cq"], stacks["ck"]
        values = {w: sb("values_" + w, [P, TT, HEADS, VW]) for w in ("sv", "cv")}
        row_max = sb("row_max", [P, 2, 3, HEADS])
        neg_max = sb("neg_max", [P, 2, 2, HEADS])
        max_t = sb("max_t", [HEADS, SEQ], f32r)
        probs = sb("probs", [P, PROBS, 2 * SEQ])
        o_un = sb("o_un", [P, 4, SEQ])
        inv = sb("inv", [P, 2, HEADS])
        o_tok = sb("o_tok", [P, 2, D])
        o_hi = sb("o_hi", [P, DK, SEQ], f32r)
        o_lo = sb("o_lo", [P, DK, SEQ], f32r)
        tanh = sb("tanh", [P, 2, TOK])
        gated = sb("gated", [P, TOK])
        hidden = sb("hidden", [P, 2, TOK])
        bn = sb("bn", [P, 2, 6])
        norms = {w: sb("norm_" + w, [P, TT, 2]) for w in ("x1", "x2", "y")}
        ve = {w: sb("ve_" + w, [P, TT]) for w in ("x1", "x2", "y")}
        rstds = {w: sb("rstd_" + w, [P, TT]) for w in ("x1", "x2", "y")}

        general = stack.enter_context(nc.psum_tensor("general", [P, 2, 512], f32))
        score = stack.enter_context(nc.psum_tensor("score", [P, 2, 512], f32))
        logit = stack.enter_context(nc.psum_tensor("logit", [P, 2, 512], f32))
        summed = stack.enter_context(nc.psum_tensor("summed", [P, 2, 512], f32))

        sem = {name: stack.enter_context(nc.semaphore(name)) for name in NAMES}
        consts_in = stack.enter_context(nc.semaphore("consts_in"))
        staged = [stack.enter_context(nc.semaphore(f"staged{n}")) for n in range(6)]
        unstaged = stack.enter_context(nc.semaphore("unstaged"))
        prepared = stack.enter_context(nc.semaphore("prepared"))
        waited = stack.enter_context(nc.semaphore("waited"))
        lot_hi = stack.enter_context(nc.semaphore("lot_hi"))
        block = stack.enter_context(nc.Block())

        def group_rows(dram, g):
            return dram.rearrange("(g t p) d -> g p t d", t=TT, p=P)[g]

        def feature_bias(what, j):
            return {"cq": b_qk[:, j:j + 1], "ck": b_qk[:, 2 + j:3 + j]}.get(what, 0.0)

        def head_index(h):
            return (h % 2) * PAIRS + h // 2

        def apart(eng):
            eng.sem_inc(waited, 1)

        def tables(eng, tally, walk):
            walk(PROLOGUE, 0, None)
            with eng.Fori(0, GROUPS - 1) as i:
                tally.enter(i)
                walk(BODY, i + 1, i)
            tally.enter(GROUPS - 1)
            walk(EPILOGUE, None, GROUPS - 1)

        stage = [values["sv"][:].rearrange("p a b c -> p (a b c)"), values["cv"][:].rearrange("p a b c -> p (a b c)")]
        LOTS = [(weights[:, 0:2048], 2048, f32), (weights[:, 2048:4096], 2048, f32), (w_gate_up[:, 0:1536], 1536, i32),
                (w_gate_up[:, 1536:3072], 1536, i32), (w_down, 1536, i32), (selectors, SELECTS, f32)]

        @block.sync
        def _(sp):
            for dst, src in ((ident, ident_in), (probs[:, 0, 0:P], mask_in), (b_qk, bias_qk), (b_vo, bias_vo)):
                sp.dma_start(dst[:], src).then_inc(consts_in, 16)
            for n, (src, cols, dt) in enumerate(LOTS):
                if n >= 2:
                    sp.wait_ge(unstaged, n - 1)
                sp.dma_start(stage[n % 2][:, 0:cols].bitcast(dt), src).then_inc(staged[n], 16)
            tally = Tally()
            sp.sem_inc(sem["stored"], 1)
            sp.dma_start(x_in[:], group_rows(x, 0)).then_inc(sem["loaded_x"], 16)
            sp.dma_start(ctx[:], group_rows(ctx_in, 0)).then_inc(sem["loaded_ctx"], 16)

            def walk(steps, front, back):
                for step in steps:
                    kind, what, n = step
                    if (kind, what, n) == ("transpose", "x", 1):
                        sp.wait_ge(sem["made"], tally.now("made") + 1)
                        apart(sp)
                        sp.wait_ge(sem["residual_x"], tally.now("residual_x"))
                        apart(sp)
                        sp.dma_start(x_in[:], group_rows(x, (front + 1) % GROUPS)).then_inc(sem["loaded_x"], 16)
                    if (kind, what, n) == ("transpose", "ctx", 1):
                        sp.wait_ge(sem["made"], tally.now("made") + 1)
                        apart(sp)
                        sp.dma_start(ctx[:], group_rows(ctx_in, (front + 1) % GROUPS)).then_inc(sem["loaded_ctx"], 16)
                    if kind == "maxima":
                        b = int(what[1])
                        q = stacks[what[0] + "q"]
                        sp.wait_ge(sem["drained_dve"], tally.now("drained_dve") + 1)
                        for s in range(2):
                            row = s * SLOT + MAX_ROW
                            sp.dma_start(q[row:row + 1, :, b * SEQ:(b + 1) * SEQ].bitcast(f32),
                                         max_t[s * PAIRS:(s + 1) * PAIRS, :].bitcast(f32)).then_inc(sem["max_sent"], 16)
                    if (kind, what[:1]) == ("norm", "y"):
                        t = 2 * int(what[1])
                        sp.wait_ge(sem["y"], tally.now("y") + 2)
                        apart(sp)
                        sp.dma_start(group_rows(out, back)[:, t:t + 2, :], r2[:, t:t + 2, :]).then_inc(sem["stored"], 16)
                    tally.passed(step)
            tables(sp, tally, walk)
            sp.wait_ge(sem["loaded_x"], tally.now("loaded_x") + 16)
            sp.wait_ge(sem["loaded_ctx"], tally.now("loaded_ctx") + 16)
            sp.wait_ge(sem["stored"], tally.now("stored") + 1)

        @block.tensor
        def _(pe):
            pe.wait_ge(consts_in, 64)
            pe.wait_ge(prepared, 1)
            tally = Tally()

            def split_matmuls(dst, lhs, rhs):
                terms = [(l, r, k) for k in range(DK) for l, r in ((lhs[0], rhs[0]), (lhs[1], rhs[0]), (lhs[0], rhs[1]))]
                for n, (l, r, k) in enumerate(terms):
                    last = nc.tensor.matmul(dst, l(k), r(k), start=(n == 0), stop=(n == len(terms) - 1))
                return last

            def walk(steps, front, back):
                drains = []
                for step in steps:
                    kind, what, n = step
                    if "made" in signals(step):
                        bank = general[:, tally.slot("made"), :]
                        if len(drains) >= 2:
                            pe.wait_ge(sem[drains[-2][0]], drains[-2][1])
                        elif steps is not PROLOGUE:
                            pe.wait_ge(sem["drained_dve"], tally.start["drained_dve"])
                            pe.wait_ge(sem["drained_act"], tally.start["drained_act"])
                        by = "drained_" + drained_by(step)
                        drains.append((by, tally.now(by) + 1))

                    if kind == "transpose":
                        src = {"x": x_in, "x1": x1, "ctx": ctx, "x2": r2}[what]
                        if what in ("x", "ctx"):
                            name = "loaded_" + what
                            pe.wait_ge(sem[name], tally.now(name) + (16 if n == 0 else 0))
                        else:
                            pe.wait_ge(sem[what], tally.now(what))
                        for tt in range(TT):
                            last = nc.tensor.transpose(bank[:, tt * P:(tt + 1) * P], src[:, tt, n * P:(n + 1) * P], ident[:])
                        last.then_inc(sem["made"], 1)

                    if kind in ("project", "value"):
                        src = {"sq": "x", "sk": "x", "sv": "x", "cq": "x1", "ck": "ctx", "cv": "ctx"}[what]
                        pe.wait_ge(sem["drained_dve"], tally.after(("transpose", src, 1), "drained_dve"))
                        w = WEIGHTS.index(what)
                        if kind == "project":
                            cols = slice(n * P, (n + 1) * P)
                            last = split_matmuls(bank,
                                                 [lambda k, w_=w_: w_[:, w, k, cols] for w_ in (w_hi, w_lo)],
                                                 [lambda k, t_=t_: t_[:, k, :] for t_ in (t_hi, t_lo)])
                        else:
                            for m in range(2):
                                tok = slice((2 * n + m) * P, (2 * n + m + 1) * P)
                                last = split_matmuls(bank[:, m * D:(m + 1) * D],
                                                     [lambda k, t_=t_: t_[:, k, tok] for t_ in (t_hi, t_lo)],
                                                     [lambda k, w_=w_: w_[:, w, k, :] for w_ in (w_hi, w_lo)])
                        last.then_inc(sem["made"], 1)

                    if kind == "stack":
                        j = n // 4
                        pe.wait_ge(sem["drained_dve"], tally.after(("project", what, j), "drained_dve"))
                        high, low = (SELECT_AT[what[1], part] + P * (n % 4) for part in ("hi", "lo"))
                        nc.tensor.matmul(bank, select[:, high:high + P], p_hi[:, j, :], start=True, stop=False)
                        nc.tensor.matmul(bank, select[:, low:low + P], p_lo[:, j, :],
                                         start=False, stop=True).then_inc(sem["made"], 1)

                    if kind == "scores":
                        b, rows, t = int(what[1]), slice((n % 2) * SLOT, (n % 2 + 1) * SLOT), n // 2
                        q, k = stacks[what[0] + "q"], stacks[what[0] + "k"]
                        base = b * SEQ
                        if n < 2 * PAIRS:
                            for w in ("q", "k"):
                                made = ("stack", what[0] + w, t)
                                by = "drained_" + drained_by(made)
                                pe.wait_ge(sem[by], tally.after(made, by))
                        wait_for(pe, sem["row_max"], tally.now("row_max") - 1)
                        bank = score[:, tally.slot("scores"), :]
                        if what[0] == "c":
                            for qt in range(2):
                                last = nc.tensor.matmul(bank[:, qt * SEQ:(qt + 1) * SEQ], q[rows, t, base + qt * P:base + (qt + 1) * P],
                                                        k[rows, t, base:base + SEQ], start=True, stop=True)
                        else:
                            nc.tensor.matmul(bank[:, 0:P], q[rows, t, base:base + P], k[rows, t, base:base + P],
                                             start=True, stop=False, skip_group_check=True)
                            nc.tensor.matmul(bank[:, P:3 * P], q[rows, t, base + P:base + 2 * P], k[rows, t, base:base + SEQ],
                                             start=False, stop=False, skip_group_check=True)
                            diagonal = bank[:, 0:4 * P].rearrange("p (a b c) -> p a b c", a=2, b=2)[:, :, 0, :]
                            last = nc.tensor.matmul(diagonal, ident_bf[:], causal[:].unsqueeze(1).broadcast_to([P, 2, P]),
                                                    start=False, stop=True, skip_group_check=True)
                        last.then_inc(sem["scores"], 1)

                    if kind == "maxima":
                        if what[0] == "s":
                            pe.wait_ge(sem["neg_max"], tally.now("neg_max") + 2)
                        else:
                            pe.wait_ge(sem["row_max"], tally.after(("scores", what, HEADS - 1), "row_max"))
                        for qt in range(2):
                            last = nc.tensor.transpose(bank[0:HEADS, qt * P:(qt + 1) * P], neg_max[:, STAGES[what] % 2, qt, :], ident[:])
                        last.then_inc(sem["made"], 1)

                    if kind == "exps":
                        b, rows, t = int(what[1]), slice((n % 2) * SLOT, (n % 2 + 1) * SLOT), n // 2
                        q, k = stacks[what[0] + "q"], stacks[what[0] + "k"]
                        base = b * SEQ
                        if n == 0:
                            pe.wait_ge(sem["max_sent"], tally.after(("maxima", what, 0), "max_sent"))
                        wait_for(pe, sem["exps"], tally.now("exps") - 1)
                        bank = logit[:, tally.slot("logits"), :]
                        nc.tensor.matmul(bank[:, 0:SEQ], k[rows, t, base:base + P], q[rows, t, base:base + SEQ], start=True, stop=True)
                        if what[0] == "c":
                            last = nc.tensor.matmul(bank[:, SEQ:2 * SEQ], k[rows, t, base + P:base + 2 * P], q[rows, t, base:base + SEQ],
                                                    start=True, stop=True)
                        else:
                            last = nc.tensor.matmul(bank[:, SEQ:SEQ + P], k[rows, t, base + P:base + 2 * P],
                                                    q[rows, t, base + P:base + 2 * P], start=True, stop=True)
                        last.then_inc(sem["logits"], 1)

                    if kind == "weigh":
                        b, v = int(what[1]), values[what[0] + "v"]
                        if n == 0:
                            for part in range(2):
                                made = ("value", what[0] + "v", part)
                                by = "drained_" + drained_by(made)
                                pe.wait_ge(sem[by], tally.after(made, by))
                        ready = "masked" if what[0] == "s" else "exps"
                        pe.wait_ge(sem[ready], tally.after(("exps", what, 4 * n + 3), ready))
                        if n % 2 == 0:
                            wait_for(pe, sem["unweighed"], tally.now("unweighed") - 1)
                        for kt in range(2):
                            first_q = P if (kt == 1 and what[0] == "s") else 0
                            for c in range(4):
                                width = SEQ - first_q
                                last = nc.tensor.matmul(summed[c * 32:(c + 1) * 32, n // 2, (n % 2) * SEQ + first_q:(n % 2 + 1) * SEQ],
                                                        v[:, 2 * b + kt, 4 * n + c, :],
                                                        probs[:, probs_slot[what, 4 * n + c], kt * SEQ:kt * SEQ + width],
                                                        start=(kt == 0), stop=(kt == 1), skip_group_check=True)
                        if n % 2 == 1:
                            last.then_inc(sem["summed"], 1)

                    if kind == "normalise":
                        pe.wait_ge(sem["unweighed"], tally.after(("weigh", what, 3), "unweighed"))
                        for g in range(4):
                            last = nc.tensor.transpose(bank[:, g * P:(g + 1) * P], o_un[:, g, n * P:(n + 1) * P], ident[:])
                        last.then_inc(sem["made"], 1)

                    if kind == "turn":
                        pe.wait_ge(sem["drained_dve"], tally.after(("normalise", what, 1), "drained_dve"))
                        for k in range(DK):
                            for tt in range(2):
                                last = nc.tensor.transpose(bank[:, k * SEQ + tt * P:k * SEQ + (tt + 1) * P],
                                                           o_tok[:, tt, k * P:(k + 1) * P], ident[:])
                        last.then_inc(sem["made"], 1)

                    if kind == "output":
                        pe.wait_ge(sem["drained_dve"], tally.after(("turn", what, 0), "drained_dve"))
                        w = WEIGHTS.index(what[0] + "o")
                        for m in range(2):
                            tok = slice(m * P, (m + 1) * P)
                            last = split_matmuls(bank[:, m * D:(m + 1) * D],
                                                 [lambda k, t_=t_: t_[:, k, tok] for t_ in (o_hi, o_lo)],
                                                 [lambda k, w_=w_: w_[:, w, k, :] for w_ in (w_hi, w_lo)])
                        last.then_inc(sem["made"], 1)

                    if kind in ("gate", "up"):
                        pe.wait_ge(sem["drained_dve"], tally.after(("transpose", "x2", 1), "drained_dve"))
                        for k in range(DK):
                            for part in (t_hi, t_lo):
                                last = nc.tensor.matmul(bank, gate_up[:, int(kind == "up"), k, n * P:(n + 1) * P], part[:, k, :],
                                                        start=(k == 0 and part is t_hi), stop=(k == DK - 1 and part is t_lo))
                        last.then_inc(sem["made"], 1)

                    if kind == "down":
                        pe.wait_ge(sem["hidden"], tally.after(("split", "", HK - 1), "hidden"))
                        for m in range(2):
                            tok = slice((2 * n + m) * P, (2 * n + m + 1) * P)
                            for k in range(HK):
                                for part in (h_hi, h_lo):
                                    last = nc.tensor.matmul(bank[:, m * D:(m + 1) * D], part[:, k, tok], down_w[:, k, :],
                                                            start=(k == 0 and part is h_hi), stop=(k == HK - 1 and part is h_lo))
                        last.then_inc(sem["made"], 1)
                    if kind == "exps":
                        probs_slot[what, n] = tally.local["exps"] % PROBS
                    tally.passed(step)
            probs_slot = {}
            tables(pe, tally, walk)

        @block.scalar
        def _(act):
            act.wait_ge(consts_in, 64)
            act.wait_ge(prepared, 1)
            tally = Tally()

            def walk(steps, front, back):
                for step in steps:
                    kind, what, n = step
                    bank = general[:, tally.slot("made"), :]
                    if kind in ("transpose", "project", "turn"):
                        act.wait_ge(sem["made"], tally.now("made") + 1)
                        if kind == "turn":
                            nc.scalar.activation(o_hi[:].rearrange("p k t -> p (k t)"), bank, ACT.Identity).then_inc(sem["high"], 1)
                        elif kind == "transpose":
                            nc.scalar.activation(t_hi[:, n, :], bank, ACT.Identity).then_inc(sem["high"], 1)
                        else:
                            nc.scalar.activation(p_hi[:, n, :], bank, ACT.Identity,
                                                 bias=feature_bias(what, n)).then_inc(sem["high"], 1)
                    if kind == "stack" and drained_by(step) == "act":
                        act.wait_ge(sem["made"], tally.now("made") + 1)
                        nc.scalar.activation(stacks[what][:, n, :], bank, ACT.Identity,
                                             bias=b_qk[:, 4:5] if what[1] == "k" else 0.0).then_inc(sem["drained_act"], 1)
                    if (kind, what) == ("value", "sv"):
                        act.wait_ge(sem["made"], tally.now("made") + 1)
                        nc.scalar.copy(values["sv"][:, 2 * n:2 * n + 2, :, 0:HD],
                                       bank.rearrange("p (t h d) -> p t h d", t=2, h=HEADS)).then_inc(sem["drained_act"], 1)
                    if kind == "exps":
                        width = 2 * SEQ if what[0] == "c" else SEQ + P
                        act.wait_ge(sem["logits"], tally.now("logits") + 1)
                        nc.scalar.activation(probs[:, tally.local["exps"] % PROBS, 0:width], logit[:, tally.slot("logits"), 0:width], ACT.Exp,
                                             scale=CROSS_SCALE if what[0] == "c" else SELF_SCALE).then_inc(sem["exps"], 1)
                    if kind == "weigh" and n % 2 == 1:
                        act.wait_ge(sem["summed"], tally.now("summed") + 1)
                        nc.scalar.copy(o_un[:, n - 1:n + 1, :],
                                       summed[:, n // 2, :].rearrange("p (g q) -> p g q", g=2)).then_inc(sem["unweighed"], 1)
                    if kind == "gate":
                        act.wait_ge(sem["made"], tally.now("made") + 1)
                        nc.scalar.activation(tanh[:, n % 2, :], bank, ACT.Tanh, scale=0.5 * QSCALE).then_inc(sem["high"], 1)
                    if kind == "split":
                        act.wait_ge(sem["drained_dve"], tally.after(("up", "", n), "drained_dve"))
                        nc.scalar.copy(h_hi[:, n, :], hidden[:, n % 2, :]).then_inc(sem["hidden_high"], 1)
                    tally.passed(step)
            tables(act, tally, walk)

        @block.vector
        def _(dve):
            dve.wait_ge(consts_in, 64)
            nc.vector.tensor_copy(ident_bf[:], ident[:])
            nc.vector.tensor_copy(causal[:], probs[:, 0, 0:P])
            nc.vector.memset(half[:], -0.5)
            w_hi2, w_lo2 = (w[:].rearrange("p a b c -> p (a b c)") for w in (w_hi, w_lo))
            gate_up2 = gate_up[:].rearrange("p a b c -> p (a b c)")
            for n, (_, cols, dt) in enumerate(LOTS):
                dve.wait_ge(staged[n], 16)
                src = stage[n % 2][:, 0:cols].bitcast(dt)
                if n < 2:
                    part = slice(n * cols, (n + 1) * cols)
                    nc.vector.tensor_copy(w_hi2[:, part], src).then_inc(lot_hi, 1)
                    dve.wait_ge(lot_hi, n + 1)
                    nc.vector.tensor_tensor(w_lo2[:, part], src, w_hi2[:, part].bitcast(f32), ALU.subtract).then_inc(unstaged, 1)
                else:
                    dst = [gate_up2[:, 0:1536], gate_up2[:, 1536:3072], down_w[:].rearrange("p k d -> p (k d)"),
                           select[:]][n - 2]
                    nc.vector.tensor_copy(dst, src).then_inc(unstaged, 1)
            dve.wait_ge(unstaged, len(LOTS))
            for n, w in enumerate(("sv", "cv")):
                nc.vector.memset(values[w][:, :, :, HD + 1:VW], 0.0)
                last = nc.vector.memset(values[w][:, :, :, HD:HD + 1], 1.0)
            last.then_inc(prepared, 1)
            tally = Tally()

            def own(ins):
                own_done[0] += 1
                ins.then_inc(sem["dve_own"], 1)
                dve.wait_ge(sem["dve_own"], tally.now("dve_own") + own_done[0])
            own_done = [0]

            def normalise_stats(rows, which, first):
                for m in range(2):
                    last = nc.vector.bn_stats(bn[:, m, :], rows[:, first + m, :])
                    if m == 1:
                        own(last)
                        apart(dve)
                for m in range(2):
                    last = nc.vector.bn_aggr(norms[which][:, first + m, :], bn[:, m, :])
                    last.then_inc(sem["stats"], 1)

            def walk(steps, front, back):
                for step in steps:
                    kind, what, n = step
                    own_done[0] = 0
                    bank = general[:, tally.slot("made"), :]
                    mine = "drained_dve" in signals(step)
                    if mine and kind != "maxima":
                        dve.wait_ge(sem["made"], tally.now("made") + 1)
                    if kind in ("transpose", "project", "turn"):
                        dve.wait_ge(sem["high"], tally.now("high") + 1)
                        if kind == "turn":
                            nc.vector.tensor_tensor(o_lo[:].rearrange("p k t -> p (k t)"), bank,
                                                    o_hi[:].rearrange("p k t -> p (k t)").bitcast(f32), ALU.subtract).then_inc(sem["drained_dve"], 1)
                        elif kind == "transpose":
                            nc.vector.tensor_tensor(t_lo[:, n, :], bank, t_hi[:, n, :].bitcast(f32), ALU.subtract).then_inc(sem["drained_dve"], 1)
                        else:
                            nc.vector.scalar_tensor_tensor(out=p_lo[:, n, :], in0=bank, scalar=feature_bias(what, n),
                                                           in1=p_hi[:, n, :].bitcast(f32), op0=ALU.add,
                                                           op1=ALU.subtract).then_inc(sem["drained_dve"], 1)
                    if kind == "stack" and mine:
                        if what[1] == "k":
                            ins = nc.vector.tensor_scalar(stacks[what][:, n, :], bank, b_qk[:, 4:5], None, ALU.add)
                        else:
                            ins = nc.vector.tensor_copy(stacks[what][:, n, :], bank)
                        ins.then_inc(sem["drained_dve"], 1)
                    if (kind, what) == ("value", "cv"):
                        nc.vector.tensor_tensor(values["cv"][:, 2 * n:2 * n + 2, :, 0:HD],
                                                bank.rearrange("p (t h d) -> p t h d", t=2, h=HEADS),
                                                b_vo[:, 0, :].rearrange("p (h d) -> p h d", h=HEADS).unsqueeze(1).broadcast_to([P, 2, HEADS, HD]),
                                                ALU.add).then_inc(sem["drained_dve"], 1)
                    if kind == "scores":
                        dve.wait_ge(sem["scores"], tally.now("scores") + 1)
                        bank, at, par = score[:, tally.slot("scores"), :], head_index(n), STAGES[what] % 2
                        if what[0] == "c":
                            nc.vector.tensor_reduce(neg_max[:, par, :, at], bank.rearrange("p (t k) -> p t k", t=2), AX, ALU.max,
                                                    negate=True).then_inc(sem["row_max"], 1)
                        else:
                            nc.vector.tensor_reduce(row_max[:, par, :, at], bank[:, 0:3 * P].rearrange("p (t k) -> p t k", t=3), AX,
                                                    ALU.max, negate=True).then_inc(sem["row_max"], 1)
                    if kind == "maxima":
                        par = STAGES[what] % 2
                        if what[0] == "s":
                            dve.wait_ge(sem["row_max"], tally.after(("scores", what, HEADS - 1), "row_max"))
                            nc.vector.tensor_copy(neg_max[:, par, 0, :], row_max[:, par, 0, :]).then_inc(sem["neg_max"], 1)
                            nc.vector.tensor_tensor(neg_max[:, par, 1, :], row_max[:, par, 1, :], row_max[:, par, 2, :],
                                                    ALU.min).then_inc(sem["neg_max"], 1)
                        dve.wait_ge(sem["made"], tally.now("made") + 1)
                        wait_for(dve, sem["max_sent"], tally.now("max_sent"))
                        nc.vector.tensor_copy(max_t[:], bank[0:HEADS, 0:SEQ]).then_inc(sem["drained_dve"], 1)
                    if kind == "normalise":
                        heads = bank.rearrange("p (h c) -> p h c", c=VW)
                        own(nc.vector.reciprocal(inv[:, n, :], heads[:, :, HD]))
                        nc.vector.tensor_tensor(o_tok[:, n, :].rearrange("p (h d) -> p h d", d=HD), heads[:, :, 0:HD],
                                                inv[:, n, :].unsqueeze(2).broadcast_to([P, HEADS, HD]), ALU.mult).then_inc(sem["drained_dve"], 1)
                    if kind == "output":
                        b, which = int(what[1]), "x1" if what[0] == "s" else "x2"
                        rows = r1 if what[0] == "s" else r2
                        res = "residual_x" if what[0] == "s" else "residual_x1"
                        dve.wait_ge(sem[res], tally.now(res))
                        ins = nc.vector.tensor_tensor(rows[:, 2 * b:2 * b + 2, :], bank.rearrange("p (t d) -> p t d", t=2),
                                                      rows[:, 2 * b:2 * b + 2, :], ALU.add)
                        ins.then_inc(sem["drained_dve"], 1)
                        dve.wait_ge(sem["drained_dve"], tally.now("drained_dve") + 1)
                        normalise_stats(rows, which, 2 * b)
                    if kind == "gate":
                        if n >= 1:
                            dve.wait_ge(sem["drained_dve"], tally.after(("up", "", n - 1), "drained_dve"))
                        dve.wait_ge(sem["high"], tally.now("high") + 1)
                        nc.vector.scalar_tensor_tensor(out=gated[:], in0=tanh[:, n % 2, :], scalar=1.0, in1=bank,
                                                       op0=ALU.add, op1=ALU.mult).then_inc(sem["drained_dve"], 1)
                    if kind == "up":
                        dve.wait_ge(sem["drained_dve"], tally.after(("gate", "", n), "drained_dve"))
                        if n >= 2:
                            dve.wait_ge(sem["hidden"], tally.after(("split", "", n - 2), "hidden"))
                        nc.vector.tensor_tensor(hidden[:, n % 2, :], gated[:], bank, ALU.mult).then_inc(sem["drained_dve"], 1)
                    if kind == "down":
                        rows = r2[:, 2 * n:2 * n + 2, :]
                        nc.vector.scalar_tensor_tensor(out=rows, in0=bank.rearrange("p (t d) -> p t d", t=2), scalar=0.5 * QSCALE ** 3,
                                                       in1=rows, op0=ALU.mult, op1=ALU.add).then_inc(sem["drained_dve"], 1)
                        dve.wait_ge(sem["drained_dve"], tally.now("drained_dve") + 1)
                        normalise_stats(r2, "y", 2 * n)
                    if kind == "norm":
                        dst, rows, which = {"s": (x1, r1, "x1"), "c": (r2, r2, "x2"), "y": (r2, r2, "y")}[what[0]]
                        made = ("down", "", int(what[1])) if what[0] == "y" else ("output", what, 0)
                        dve.wait_ge(sem["rstd"], tally.after(made, "rstd"))
                        for t in range(2 * int(what[1]), 2 * int(what[1]) + 2):
                            nc.vector.tensor_scalar(dst[:, t, :], rows[:, t, :], norms[which][:, t, 0:1], rstds[which][:, t:t + 1],
                                                    ALU.subtract, ALU.mult).then_inc(sem[which], 1)
                    tally.passed(step)
            tables(dve, tally, walk)

        @block.gpsimd
        def _(pool):
            pool.wait_ge(prepared, 1)
            tally = Tally()

            def own(ins):
                own_done[0] += 1
                ins.then_inc(sem["pool_own"], 1)
                pool.wait_ge(sem["pool_own"], tally.now("pool_own") + own_done[0])
                apart(pool)
            own_done = [0]

            def inverse_deviation(which, first):
                pool.wait_ge(sem["stats"], tally.now("stats") + 2)
                apart(pool)
                v, two = ve[which], slice(first, first + 2)
                own(nc.gpsimd.tensor_scalar(v[:, two], norms[which][:, two, 1], EPS, None, ALU.add))
                nc.gpsimd.tensor_tensor(rstds[which][:, two], v[:, two], half[:], ALU.pow).then_inc(sem["rstd"], 1)

            def walk(steps, front, back):
                for step in steps:
                    kind, what, n = step
                    own_done[0] = 0
                    if (kind, n) == ("transpose", 0) and what == "x":
                        pool.wait_ge(sem["loaded_x"], tally.now("loaded_x") + 16)
                        wait_for(pool, sem["x1"], tally.now("x1"))
                        apart(pool)
                        nc.gpsimd.tensor_copy(r1[:], x_in[:]).then_inc(sem["residual_x"], 1)
                    if (kind, n) == ("transpose", 0) and what == "x1":
                        pool.wait_ge(sem["x1"], tally.now("x1"))
                        pool.wait_ge(sem["stored"], tally.now("stored") + 1)
                        apart(pool)
                        nc.gpsimd.tensor_tensor(r2[:], x1[:], b_vo[:, 1, :].unsqueeze(1).broadcast_to([P, TT, D]),
                                                ALU.add).then_inc(sem["residual_x1"], 1)
                    if kind == "exps" and what[0] == "s":
                        pool.wait_ge(sem["exps"], tally.now("exps") + 1)
                        apart(pool)
                        blocks = probs[:, tally.local["exps"] % PROBS, :].rearrange("p (a b) -> p a b", a=2)[:, :, 0:P]
                        nc.gpsimd.affine_select(out=blocks, in_=blocks, compare_op=ALU.is_ge, fill=0.0, base=0,
                                                pattern=[[0, 2], [1, P]], channel_multiplier=-1).then_inc(sem["masked"], 1)
                    if kind == "output":
                        inverse_deviation("x1" if what[0] == "s" else "x2", 2 * int(what[1]))
                    if kind == "down":
                        inverse_deviation("y", 2 * n)
                    if kind == "split":
                        pool.wait_ge(sem["hidden_high"], tally.now("hidden_high") + 1)
                        apart(pool)
                        nc.gpsimd.tensor_tensor(h_lo[:, n, :], hidden[:, n % 2, :], h_hi[:, n, :].bitcast(f32),
                                                ALU.subtract).then_inc(sem["hidden"], 1)
                    tally.passed(step)
            tables(pool, tally, walk)


def _constants():
    import numpy as np
    places = {("q", "hi"): (0, 1), ("q", "lo"): (2,), ("k", "hi"): (1, 2), ("k", "lo"): (0,)}
    sel = np.zeros((P, SELECTS), np.float32)
    for which, blocks in places.items():
        for head in range(P // HD):
            for d in range(HD):
                for blk in blocks:
                    sel[head * HD + d, SELECT_AT[which] + head // 2 * P + head % 2 * SLOT + blk * HD + d] = 1.0
    row = np.arange(P)
    mask = np.where(row[None, :] > row[:, None], MASKED, 0.0).astype(np.float32)
    one_row = (row % SLOT == MAX_ROW).astype(np.float32)[:, None]
    return sel, np.eye(P, dtype=np.float32), mask, one_row


def kernel(**inputs):
    import numpy as np
    import concourse.bacc as _bacc
    from concourse import mybir as _mybir
    from concourse.bass_utils import run_bass_kernel_spmd as _run

    a = {name: np.asarray(v) for name, v in inputs.items()}

    def rows(w):
        return w.reshape(-1, P, w.shape[1]).transpose(1, 0, 2)

    qkv = a["L0_attn_w_qkv"].reshape(D, HEADS, 3, HD).transpose(2, 0, 1, 3).reshape(3, D, D)
    mats = [qkv[0], qkv[1], qkv[2], a["L0_attn_w_o"]] + [a["L0_xattn_W" + n].T for n in "qkvo"]
    weights = np.stack([rows(m) for m in mats], 1).reshape(P, -1)
    gate_up = np.stack([rows(a["L0_ffn_w_gate"].T), rows(a["L0_ffn_w_up"].T)], 1).reshape(P, -1)
    down = rows(a["L0_ffn_w_down"].T).reshape(P, -1)
    sel, eye, mask, one_row = _constants()
    bias_qk = np.concatenate([a["L0_xattn_bq"].reshape(2, P).T, a["L0_xattn_bk"].reshape(2, P).T, one_row], 1)
    bias_vo = np.broadcast_to(np.stack([a["L0_xattn_bv"], a["L0_xattn_bo"]])[None], (P, 2, D))
    laid = {"x": a["x"].reshape(SEQS * SEQ, D), "ctx": a["ctx_1024"].reshape(SEQS * SEQ, D), "weights": weights,
            "gate_up": gate_up, "down": down, "bias_qk": bias_qk, "bias_vo": bias_vo, "selectors": sel, "ident": eye, "mask": mask}

    nc = _bacc.Bacc("TRN2", target_bir_lowering=False, num_devices=1)
    nc.disable_value_cache = True
    arrays, args = {}, []
    for name, value in laid.items():
        value = np.ascontiguousarray(value)
        arrays[name + "_dram"] = value
        args.append(nc.dram_tensor(name + "_dram", value.shape, _mybir.dt.from_np(value.dtype), kind="ExternalInput").ap())
    y = nc.dram_tensor("y_dram", (SEQS * SEQ, D), _mybir.dt.float32, kind="ExternalOutput").ap()
    decoder_layer(nc, *args, y)
    r = _run(nc, [arrays], core_ids=[0])
    return r.results[0]["y_dram"].reshape(SEQS, SEQ, D)
```

```python
from contextlib import ExitStack

import concourse.bass as bass
from concourse import mybir

P = 128
SEQS, SEQ, D = 16, 256, 256
HEADS, HD = 16, 16
HIDDEN = 768
GROUP = 2
TOK = GROUP * SEQ
TT = TOK // P
GROUPS = SEQS // GROUP
DK = D // P
HK = HIDDEN // P
PAIRS = HEADS // 2
SLOT = P // 2
MAX_ROW = 3 * HD
VW = 32
SELECT_AT = {("q", "hi"): HD, ("k", "hi"): 0, ("q", "lo"): 4 * P + HD, ("k", "lo"): 4 * P + 3 * HD}
SELECTS = 8 * P + 3 * HD
EPS = 1e-5
MASKED = -1e30
QSCALE = 1.0 / 127.0
SELF_SCALE = 1.0 / 16.0
CROSS_SCALE = 1.0 / 4.0
WEIGHTS = ["sq", "sk", "sv", "so", "cq", "ck", "cv", "co"]
BANKS = 3
PROBS = 6
SCORE_LEAD = 23
PROLOGUE_LEAD = 22
EPILOGUE_LEAD = 22
WEIGH_LAG = 2
MAXIMA_AT = 2
BODY_AT = (1, 4, 7, 8, 10, 3)
PROLOGUE_AT = (1, 5, 8, 9, 12, 0)
EPILOGUE_AT = (1, 3, 6, 8, 10, 4)
CTX_AT = 12
PRODUCTS_LEAD = 2
X2_WAIT = (2, 0)
HALVES_APART = 1
HELD = ("normalise",)
KEYS_BY_ACT = (("ck", 1), ("ck", 3))
STAGES = {"c0": 0, "c1": 1, "s0": 2, "s1": 3}


def stacks_of(what, first=0, last=PAIRS):
    return [("stack", what, t) for t in range(first, last)]


X_SIDE = ([("transpose", "x", 0), ("transpose", "x", 1), ("project", "sq", 0), ("project", "sq", 1), ("value", "sv", 0)]
          + stacks_of("sq") + [("project", "sk", 0), ("project", "sk", 1), ("value", "sv", 1)] + stacks_of("sk", 0, 1))
CTX_SIDE = [("transpose", "ctx", 0), ("transpose", "ctx", 1)]
CTX_PRODUCTS = [("value", "cv", 0), ("value", "cv", 1), ("project", "ck", 0), None, None, ("project", "ck", 1)]
NORM_Y = [("norm", "y0", 0), ("norm", "y1", 0)]
FIRST_KEYS = stacks_of("ck", 0, 1)
X1_TURNED = [("transpose", "x1", 0), ("transpose", "x1", 1)]
X1_SIDE = [("residual", "x1", 0)] + stacks_of("ck", 1) + [("project", "cq", 0), ("project", "cq", 1)]
BOTH_SIDES = (stacks_of("cq", 2, 3) + [("transpose", "x", 1)] + stacks_of("cq", 3, 6)
              + [("project", "sq", 0)] + stacks_of("cq", 6, 7) + [("value", "sv", 0)]
              + stacks_of("cq", 7, 8) + [("project", "sq", 1)]
              + stacks_of("sq") + [("project", "sk", 0), ("project", "sk", 1), ("value", "sv", 1)] + stacks_of("sk"))


def before(b, k, n):
    return (b * HK + k - n) // HK, (b * HK + k - n) % HK


def ffn_half(b):
    steps = [("transpose", "x2", b)] + [None] * X2_WAIT[b]
    for k in range(HK):
        steps += [("gate", b, k), ("up", b, k)]
        if (b, k) != (0, 0):
            steps.append(("split",) + before(b, k, 1))
    return steps


FFN = ffn_half(0) + [None] * HALVES_APART + ffn_half(1)
LAST_SPLIT = [("split", 1, HK - 1)]
DOWN = [("down", "", 0), ("stats", "y0", 0), ("down", "", 1)]
FREE = ("split", "norm", "gather", "residual", "stats")


def attention_steps(stages, early, late, products=(), lead=SCORE_LEAD, at=BODY_AT):
    normalise_at, turn_at, output_at, stats_at, norm_at, ffn_at = at
    steps, total, late_from = [], HEADS * len(stages), None
    early, late, products = list(early), list(late), list(products)
    end = total + lead + WEIGH_LAG
    for n in range(end + norm_at):
        if n < total:
            steps.append(("scores", stages[n // HEADS], n % HEADS))
        if n < total and n % HEADS == HEADS - 1 and stages[n // HEADS][0] == "s":
            steps.append(("gather", stages[n // HEADS], 0))
        j = (n - HEADS - MAXIMA_AT) // HEADS
        if n >= HEADS + MAXIMA_AT and (n - HEADS - MAXIMA_AT) % HEADS == 0 and j < len(stages):
            steps.append(("maxima", stages[j], 0))
        m = n - lead
        if 0 <= m < total:
            steps.append(("exps", stages[m // HEADS], m % HEADS))
        w = m - WEIGH_LAG
        if 0 <= w < total and w % 4 == 3:
            steps.append(("weigh", stages[w // HEADS], w % HEADS // 4))
        j, after = (w - (HEADS - 1)) // HEADS, (w - (HEADS - 1)) % HEADS
        if w >= HEADS - 1 and j < len(stages):
            st = stages[j]
            if after == normalise_at:
                steps += [("normalise", st, 0), ("normalise", st, 1)]
            if after == turn_at:
                steps.append(("turn", st, 0))
            if after == output_at:
                steps.append(("output", st, 0))
            if after == stats_at:
                steps.append(("stats", st, 0))
            if after == norm_at:
                steps.append(("norm", st, 0))
                if st == "c0":
                    late_from = n + ffn_at
        if early:
            steps.append(early.pop(0))
        elif late and late_from is not None and n >= late_from:
            steps.append(late.pop(0))
            while late and late[0] and late[0][0] in FREE:
                steps.append(late.pop(0))
        if products and n >= end - PRODUCTS_LEAD:
            steps.append(products.pop(0))
    return [step for step in steps + late if step]


def drained_by(step):
    kind, what, n = step
    if kind == "stack":
        return "act" if what[1] == "q" or n % 2 == 0 or (what, n) in KEYS_BY_ACT else "dve"
    return "act" if (kind, what) == ("value", "sv") else "dve"


def signals(step):
    kind, what, n = step
    out = {}
    if kind not in FREE + ("scores", "exps", "weigh"):
        out["made"] = 1
        out["drained_" + drained_by(step)] = 1
    if kind in ("transpose", "project", "turn", "gate"):
        out["high"] = 1
    if kind == "scores":
        out["scores"] = out["row_max"] = 1
    if kind == "maxima":
        out["max_sent"] = 32
    if kind == "gather":
        out["neg_max"] = 2
    if kind == "exps":
        out["logits"] = out["exps"] = 1
        out["masked"] = 1 if what[0] == "s" else 0
    if kind == "weigh":
        out["summed"] = out["unweighed"] = 1
    if kind == "normalise":
        out["dve_own"] = 1
    if kind == "stats":
        out["dve_own"], out["stats"], out["pool_own"], out["rstd"] = 1, 2, 1, 1
    if kind == "norm":
        out[{"s": "x1", "c": "x2", "y": "y"}[what[0]]] = 2
    if kind == "split":
        out["hidden_high"] = out["hidden"] = 1
    if kind == "norm" and what[0] == "y":
        out["stored"] = 16
    if kind == "residual" or (kind, what, n) == ("transpose", "x", 0):
        out["residual_" + what] = 1
    if (kind, n) == ("transpose", 0) and what in ("x", "ctx"):
        out["loaded_" + what] = 16
    return out


PROLOGUE = (X_SIDE
            + attention_steps(["s0", "s1"], stacks_of("sk", 1) + [None] * CTX_AT + CTX_SIDE + [p for p in CTX_PRODUCTS if p],
                              [], lead=PROLOGUE_LEAD, at=PROLOGUE_AT)
            + X1_TURNED + FIRST_KEYS)
BODY = (X1_SIDE + [("transpose", "x", 0)] + stacks_of("cq", 0, 2)
        + attention_steps(["c0", "c1", "s0", "s1"], BOTH_SIDES, FFN + CTX_SIDE + LAST_SPLIT, CTX_PRODUCTS)
        + DOWN + X1_TURNED + [("stats", "y1", 0)] + FIRST_KEYS + NORM_Y)
EPILOGUE = (X1_SIDE + stacks_of("cq", 0, 2)
            + attention_steps(["c0", "c1"], stacks_of("cq", 2), FFN + LAST_SPLIT, lead=EPILOGUE_LEAD, at=EPILOGUE_AT)
            + DOWN + [("stats", "y1", 0)] + NORM_Y)
NAMES = sorted({name for table in (BODY, EPILOGUE) for step in table for name in signals(step)})


LAST_MADE = [s for s in BODY if "made" in signals(s)][-BANKS:]
assert LAST_MADE == [s for s in PROLOGUE if "made" in signals(s)][-BANKS:]


def signalled(steps, name):
    return sum(signals(s).get(name, 0) for s in steps)


class Tally:

    def __init__(self):
        self.start = {name: 0 for name in NAMES}
        self.local = dict(self.start)
        self.marks = {}
        self.first_bank = -signalled(PROLOGUE, "made") % BANKS

    def enter(self, turn, table):
        self.marks = {}
        self.first_bank = -signalled(table, "made") % BANKS
        for name in NAMES:
            self.start[name] = turn * signalled(BODY, name) + signalled(PROLOGUE, name)
            self.local[name] = 0

    def now(self, name):
        return self.start[name] + self.local[name]

    def passed(self, step):
        for name, n in signals(step).items():
            self.local[name] += n
            self.marks[step, name] = self.now(name)

    def after(self, step, name):
        if (step, name) in self.marks:
            return self.marks[step, name]
        return self.start[name] - min(signalled(table[table.index(step) + 1:], name) if step in table else 0
                                      for table in (PROLOGUE, BODY))

    def slot(self, name):
        return self.local[name] % 2

    def bank(self):
        return (self.first_bank + self.local["made"]) % BANKS


def vector_order(steps):
    out, held = [], []
    for step in steps:
        if step[0] in ("transpose", "project", "turn") + HELD:
            held.append(step)
        elif step[0] in ("exps", "weigh"):
            out.append(step)
        else:
            out += [step] + held if step[0] == "scores" else held + [step]
            held = []
    return out + held


def wait_for(eng, sem, value):
    if not (isinstance(value, int) and value <= 0):
        eng.wait_ge(sem, value)


def decoder_layer(nc, x, ctx_in, weights, w_gate_up, w_down, bias_qk, bias_vo, selectors, ident_in, mask_in, out):
    f32, f32r, bf16, i32 = mybir.dt.float32, mybir.dt.float32r, mybir.dt.bfloat16, mybir.dt.int32
    ALU, ACT, AX = mybir.AluOpType, mybir.ActivationFunctionType, mybir.AxisListType.X

    stack = ExitStack()
    with stack:
        def sb(name, shape, dt=f32):
            return stack.enter_context(nc.sbuf_tensor(name, shape, dt))

        w_hi = sb("w_hi", [P, len(WEIGHTS), DK, D], f32r)
        w_lo = sb("w_lo", [P, len(WEIGHTS), DK, D], f32r)
        gate_up = sb("gate_up", [P, 2, DK, HIDDEN], f32r)
        down_w = sb("down_w", [P, HK, D], f32r)
        select = sb("select", [P, SELECTS], f32r)
        ident = sb("ident", [P, P])
        ident_bf = sb("ident_bf", [P, P], bf16)
        causal = sb("causal", [P, P], bf16)
        b_qk = sb("b_qk", [P, 5])
        b_vo = sb("b_vo", [P, 2, D])
        half = sb("half", [P, 2])
        x_in = sb("x_in", [P, TT, D])
        ctx = sb("ctx", [P, TT, D])
        r1 = sb("r1", [P, TT, D])
        x1 = sb("x1", [P, TT, D])
        r2 = sb("r2", [P, TT, D])
        t_hi = sb("t_hi", [P, DK, TOK], f32r)
        t_lo = sb("t_lo", [P, DK, TOK], f32r)
        p_hi = sb("p_hi", [P, DK, TOK], f32r)
        p_lo = sb("p_lo", [P, DK, TOK], f32r)
        stacks = {w: sb("stack_" + w, [P, PAIRS, TOK], f32r) for w in ("sq", "sk", "cq", "ck")}
        h_hi, h_lo = stacks["cq"], stacks["ck"]
        values = {w: sb("values_" + w, [P, TT, HEADS, VW]) for w in ("sv", "cv")}
        row_max = sb("row_max", [P, 2, 3, HEADS])
        neg_max = sb("neg_max", [P, 2, 2, HEADS])
        max_t = sb("max_t", [HEADS, SEQ], f32r)
        probs = sb("probs", [P, PROBS, 2 * SEQ])
        o_un = sb("o_un", [P, 4, SEQ])
        inv = sb("inv", [P, 2, HEADS])
        o_tok = sb("o_tok", [P, 2, D])
        o_hi = sb("o_hi", [P, DK, SEQ], f32r)
        o_lo = sb("o_lo", [P, DK, SEQ], f32r)
        tanh = sb("tanh", [P, 2, TOK])
        gated = sb("gated", [P, TOK])
        hidden = sb("hidden", [P, 2, TOK])
        bn = sb("bn", [P, 2, 6])
        norms = {w: sb("norm_" + w, [P, TT, 2]) for w in ("x1", "x2", "y")}
        ve = {w: sb("ve_" + w, [P, TT]) for w in ("x1", "x2", "y")}
        rstds = {w: sb("rstd_" + w, [P, TT]) for w in ("x1", "x2", "y")}

        general = stack.enter_context(nc.psum_tensor("general", [P, BANKS, 512], f32))
        score = stack.enter_context(nc.psum_tensor("score", [P, 2, 512], f32))
        logit = stack.enter_context(nc.psum_tensor("logit", [P, 2, 512], f32))
        summed = stack.enter_context(nc.psum_tensor("summed", [P, 2, SEQ], f32))

        sem = {name: stack.enter_context(nc.semaphore(name)) for name in NAMES}
        arrived = {name: stack.enter_context(nc.semaphore("arrived_" + name))
                   for name in ("queries_keys", "small", "tables", "values_out", "bias_vo") + tuple(f"later{n}" for n in range(7))}
        prepared = stack.enter_context(nc.semaphore("prepared"))
        cross_read = stack.enter_context(nc.semaphore("cross_read"))
        pool_ready = stack.enter_context(nc.semaphore("pool_ready"))
        waited = stack.enter_context(nc.semaphore("waited"))
        first_hi = stack.enter_context(nc.semaphore("first_hi"))
        later_hi = stack.enter_context(nc.semaphore("later_hi"))
        block = stack.enter_context(nc.Block())

        def group_rows(dram, g):
            return dram.rearrange("(g t p) d -> g p t d", t=TT, p=P)[g]

        def feature_bias(what, j):
            return {"cq": b_qk[:, j:j + 1], "ck": b_qk[:, 2 + j:3 + j]}.get(what, 0.0)

        def turned(t, bank, what, n):
            if what == "x2":
                return t[:, :, n * SEQ:(n + 1) * SEQ], bank.rearrange("p (k t) -> p k t", k=DK)
            return t[:, n, :], bank

        def head_index(h):
            return (h % 2) * PAIRS + h // 2

        def apart(eng):
            eng.sem_inc(waited, 1)

        def tables(eng, tally, walk, order=list):
            walk(order(PROLOGUE), 0, None)
            with eng.Fori(0, GROUPS - 1) as i:
                tally.enter(i, BODY)
                walk(order(BODY), i + 1, i)
            tally.enter(GROUPS - 1, EPILOGUE)
            walk(order(EPILOGUE), None, GROUPS - 1)

        def flat(t):
            return t[:].rearrange("p a b c -> p (a b c)") if len(t.shape) == 4 else t[:].rearrange("p a b -> p (a b)")
        w_hi2, w_lo2 = flat(w_hi), flat(w_lo)
        WCOLS = DK * D
        stage_self = flat(values["cv"])[:, 0:4 * WCOLS]
        stage_tables = flat(probs)[:, 0:P + SELECTS]
        half_lot = 2 * WCOLS
        LATER = [(flat(x1), weights[:, 4 * WCOLS:6 * WCOLS], w_hi2[:, 4 * WCOLS:6 * WCOLS]),
                 (flat(r2), weights[:, 6 * WCOLS:], w_hi2[:, 6 * WCOLS:]),
                 (flat(tanh), w_gate_up[:, 0:half_lot], flat(gate_up)[:, 0:half_lot]),
                 (flat(hidden), w_gate_up[:, half_lot:2 * half_lot], flat(gate_up)[:, half_lot:2 * half_lot]),
                 (gated[:], w_down[:, half_lot:], flat(down_w)[:, half_lot:]),
                 (flat(x1), w_gate_up[:, 2 * half_lot:], flat(gate_up)[:, 2 * half_lot:]),
                 (flat(r2), w_down[:, 0:half_lot], flat(down_w)[:, 0:half_lot])]

        @block.sync
        def _(sp):
            sp.dma_start(stage_self[:, 0:2 * WCOLS], weights[:, 0:2 * WCOLS]).then_inc(arrived["queries_keys"], 16)
            sp.dma_start(x_in[:], group_rows(x, 0)).then_inc(sem["loaded_x"], 16)
            sp.dma_start(ident[:], ident_in).then_inc(arrived["small"], 16)
            sp.dma_start(b_qk[:], bias_qk).then_inc(arrived["small"], 16)
            sp.dma_start(stage_tables[:, P:], selectors).then_inc(arrived["tables"], 16)
            sp.dma_start(stage_tables[:, 0:P], mask_in).then_inc(arrived["tables"], 16)
            sp.dma_start(stage_self[:, 2 * WCOLS:], weights[:, 2 * WCOLS:4 * WCOLS]).then_inc(arrived["values_out"], 16)
            sp.dma_start(b_vo[:], bias_vo).then_inc(arrived["bias_vo"], 16)
            sp.dma_start(ctx[:], group_rows(ctx_in, 0)).then_inc(sem["loaded_ctx"], 16)
            for n, (lot, src, _) in enumerate(LATER):
                if n >= 5:
                    sp.wait_ge(cross_read, n - 4)
                sp.dma_start(lot if n < 2 else lot.bitcast(i32), src).then_inc(arrived[f"later{n}"], 16)
            tally = Tally()
            sp.sem_inc(sem["stored"], 1)

            def walk(steps, front, back):
                for step in steps:
                    kind, what, n = step
                    if (kind, what, n) == ("transpose", "x", 1):
                        sp.wait_ge(sem["made"], tally.now("made") + 1)
                        apart(sp)
                        sp.wait_ge(sem["residual_x"], tally.now("residual_x"))
                        apart(sp)
                        sp.dma_start(x_in[:], group_rows(x, (front + 1) % GROUPS)).then_inc(sem["loaded_x"], 16)
                    if (kind, what, n) == ("transpose", "ctx", 1):
                        sp.wait_ge(sem["made"], tally.now("made") + 1)
                        apart(sp)
                        sp.dma_start(ctx[:], group_rows(ctx_in, (front + 1) % GROUPS)).then_inc(sem["loaded_ctx"], 16)
                    if kind == "maxima":
                        b = int(what[1])
                        q = stacks[what[0] + "q"]
                        sp.wait_ge(sem["drained_dve"], tally.now("drained_dve") + 1)
                        for s in range(2):
                            row = s * SLOT + MAX_ROW
                            sp.dma_start(q[row:row + 1, :, b * SEQ:(b + 1) * SEQ].bitcast(f32),
                                         max_t[s * PAIRS:(s + 1) * PAIRS, :].bitcast(f32)).then_inc(sem["max_sent"], 16)
                    if kind == "norm" and what[0] == "y":
                        t = 2 * int(what[1])
                        sp.wait_ge(sem["y"], tally.now("y") + 2)
                        apart(sp)
                        sp.dma_start(group_rows(out, back)[:, t:t + 2, :], r2[:, t:t + 2, :]).then_inc(sem["stored"], 16)
                    tally.passed(step)
            tables(sp, tally, walk)
            sp.wait_ge(sem["loaded_x"], tally.now("loaded_x") + 16)
            sp.wait_ge(sem["loaded_ctx"], tally.now("loaded_ctx") + 16)
            sp.wait_ge(sem["stored"], tally.now("stored") + 1)

        @block.tensor
        def _(pe):
            pe.wait_ge(arrived["small"], 32)
            tally = Tally()

            def split_matmuls(dst, lhs, rhs):
                terms = [(l, r, k) for k in range(DK) for l, r in ((lhs[0], rhs[0]), (lhs[1], rhs[0]), (lhs[0], rhs[1]))]
                for n, (l, r, k) in enumerate(terms):
                    last = nc.tensor.matmul(dst, l(k), r(k), start=(n == 0), stop=(n == len(terms) - 1))
                return last

            def walk(steps, front, back):
                holder = dict(enumerate(LAST_MADE if back is not None else [None] * BANKS))
                for step in steps:
                    kind, what, n = step
                    if back is None:
                        if step == ("project", "sq", 0):
                            pe.wait_ge(prepared, 1)
                        uses = {("value", "sv", 0): 1, ("output", "s0", 0): 2, ("output", "s1", 0): 3}
                        if step == ("value", "cv", 0):
                            pe.wait_ge(cross_read, 2)
                        if step in uses:
                            pe.wait_ge(pool_ready, uses[step])
                    if "made" in signals(step):
                        bank, held = general[:, tally.bank(), :], holder[tally.bank()]
                        if held:
                            by = "drained_" + drained_by(held)
                            pe.wait_ge(sem[by], tally.after(held, by))
                        holder[tally.bank()] = step

                    if kind == "transpose":
                        src = {"x": x_in, "x1": x1, "ctx": ctx, "x2": r2}[what]
                        if what in ("x", "ctx"):
                            name = "loaded_" + what
                            pe.wait_ge(sem[name], tally.now(name) + (16 if n == 0 else 0))
                        else:
                            pe.wait_ge(sem[what], tally.now(what))
                        for tt in range(TT):
                            if what == "x2":
                                k, tok = tt // 2, 2 * n + tt % 2
                                last = nc.tensor.transpose(bank[:, tt * P:(tt + 1) * P], src[:, tok, k * P:(k + 1) * P], ident[:])
                            else:
                                last = nc.tensor.transpose(bank[:, tt * P:(tt + 1) * P], src[:, tt, n * P:(n + 1) * P], ident[:])
                        last.then_inc(sem["made"], 1)

                    if kind in ("project", "value"):
                        src = {"sq": "x", "sk": "x", "sv": "x", "cq": "x1", "ck": "ctx", "cv": "ctx"}[what]
                        pe.wait_ge(sem["drained_dve"], tally.after(("transpose", src, 1), "drained_dve"))
                        w = WEIGHTS.index(what)
                        if kind == "project":
                            cols = slice(n * P, (n + 1) * P)
                            last = split_matmuls(bank,
                                                 [lambda k, w_=w_: w_[:, w, k, cols] for w_ in (w_hi, w_lo)],
                                                 [lambda k, t_=t_: t_[:, k, :] for t_ in (t_hi, t_lo)])
                        else:
                            for m in range(2):
                                tok = slice((2 * n + m) * P, (2 * n + m + 1) * P)
                                last = split_matmuls(bank[:, m * D:(m + 1) * D],
                                                     [lambda k, t_=t_: t_[:, k, tok] for t_ in (t_hi, t_lo)],
                                                     [lambda k, w_=w_: w_[:, w, k, :] for w_ in (w_hi, w_lo)])
                        last.then_inc(sem["made"], 1)

                    if kind == "stack":
                        j = n // 4
                        pe.wait_ge(sem["drained_dve"], tally.after(("project", what, j), "drained_dve"))
                        high, low = (SELECT_AT[what[1], part] + P * (n % 4) for part in ("hi", "lo"))
                        nc.tensor.matmul(bank, select[:, high:high + P], p_hi[:, j, :], start=True, stop=False)
                        nc.tensor.matmul(bank, select[:, low:low + P], p_lo[:, j, :],
                                         start=False, stop=True).then_inc(sem["made"], 1)

                    if kind == "scores":
                        b, rows, t = int(what[1]), slice((n % 2) * SLOT, (n % 2 + 1) * SLOT), n // 2
                        q, k = stacks[what[0] + "q"], stacks[what[0] + "k"]
                        base = b * SEQ
                        if n < 2 * PAIRS:
                            for w in ("q", "k"):
                                made = ("stack", what[0] + w, t)
                                by = "drained_" + drained_by(made)
                                pe.wait_ge(sem[by], tally.after(made, by))
                        wait_for(pe, sem["row_max"], tally.now("row_max") - 1)
                        bank = score[:, tally.slot("scores"), :]
                        if what[0] == "c":
                            for qt in range(2):
                                last = nc.tensor.matmul(bank[:, qt * SEQ:(qt + 1) * SEQ], q[rows, t, base + qt * P:base + (qt + 1) * P],
                                                        k[rows, t, base:base + SEQ], start=True, stop=True)
                        else:
                            nc.tensor.matmul(bank[:, 0:P], q[rows, t, base:base + P], k[rows, t, base:base + P],
                                             start=True, stop=False, skip_group_check=True)
                            nc.tensor.matmul(bank[:, P:3 * P], q[rows, t, base + P:base + 2 * P], k[rows, t, base:base + SEQ],
                                             start=False, stop=False, skip_group_check=True)
                            diagonal = bank[:, 0:4 * P].rearrange("p (a b c) -> p a b c", a=2, b=2)[:, :, 0, :]
                            last = nc.tensor.matmul(diagonal, ident_bf[:], causal[:].unsqueeze(1).broadcast_to([P, 2, P]),
                                                    start=False, stop=True, skip_group_check=True)
                        last.then_inc(sem["scores"], 1)

                    if kind == "maxima":
                        if what[0] == "s":
                            pe.wait_ge(sem["neg_max"], tally.after(("gather", what, 0), "neg_max"))
                        else:
                            pe.wait_ge(sem["row_max"], tally.after(("scores", what, HEADS - 1), "row_max"))
                        for qt in range(2):
                            last = nc.tensor.transpose(bank[0:HEADS, qt * P:(qt + 1) * P], neg_max[:, STAGES[what] % 2, qt, :], ident[:])
                        last.then_inc(sem["made"], 1)

                    if kind == "exps":
                        b, rows, t = int(what[1]), slice((n % 2) * SLOT, (n % 2 + 1) * SLOT), n // 2
                        q, k = stacks[what[0] + "q"], stacks[what[0] + "k"]
                        base = b * SEQ
                        if n == 0:
                            pe.wait_ge(sem["max_sent"], tally.after(("maxima", what, 0), "max_sent"))
                        wait_for(pe, sem["exps"], tally.now("exps") - 1)
                        bank = logit[:, tally.slot("logits"), :]
                        nc.tensor.matmul(bank[:, 0:SEQ], k[rows, t, base:base + P], q[rows, t, base:base + SEQ], start=True, stop=True)
                        if what[0] == "c":
                            last = nc.tensor.matmul(bank[:, SEQ:2 * SEQ], k[rows, t, base + P:base + 2 * P], q[rows, t, base:base + SEQ],
                                                    start=True, stop=True)
                        else:
                            last = nc.tensor.matmul(bank[:, SEQ:SEQ + P], k[rows, t, base + P:base + 2 * P],
                                                    q[rows, t, base + P:base + 2 * P], start=True, stop=True)
                        last.then_inc(sem["logits"], 1)

                    if kind == "weigh":
                        b, v = int(what[1]), values[what[0] + "v"]
                        if n == 0:
                            for part in range(2):
                                made = ("value", what[0] + "v", part)
                                by = "drained_" + drained_by(made)
                                pe.wait_ge(sem[by], tally.after(made, by))
                        ready = "masked" if what[0] == "s" else "exps"
                        pe.wait_ge(sem[ready], tally.after(("exps", what, 4 * n + 3), ready))
                        wait_for(pe, sem["unweighed"], tally.now("unweighed") - 1)
                        for kt in range(2):
                            first_q = P if (kt == 1 and what[0] == "s") else 0
                            for c in range(4):
                                width = SEQ - first_q
                                last = nc.tensor.matmul(summed[c * 32:(c + 1) * 32, n % 2, first_q:SEQ],
                                                        v[:, 2 * b + kt, 4 * n + c, :],
                                                        probs[:, probs_slot[what, 4 * n + c], kt * SEQ:kt * SEQ + width],
                                                        start=(kt == 0), stop=(kt == 1), skip_group_check=True)
                        last.then_inc(sem["summed"], 1)

                    if kind == "normalise":
                        pe.wait_ge(sem["unweighed"], tally.after(("weigh", what, 3), "unweighed"))
                        for g in range(4):
                            last = nc.tensor.transpose(bank[:, g * P:(g + 1) * P], o_un[:, g, n * P:(n + 1) * P], ident[:])
                        last.then_inc(sem["made"], 1)

                    if kind == "turn":
                        pe.wait_ge(sem["drained_dve"], tally.after(("normalise", what, 1), "drained_dve"))
                        for k in range(DK):
                            for tt in range(2):
                                last = nc.tensor.transpose(bank[:, k * SEQ + tt * P:k * SEQ + (tt + 1) * P],
                                                           o_tok[:, tt, k * P:(k + 1) * P], ident[:])
                        last.then_inc(sem["made"], 1)

                    if kind == "output":
                        pe.wait_ge(sem["drained_dve"], tally.after(("turn", what, 0), "drained_dve"))
                        w = WEIGHTS.index(what[0] + "o")
                        for m in range(2):
                            tok = slice(m * P, (m + 1) * P)
                            last = split_matmuls(bank[:, m * D:(m + 1) * D],
                                                 [lambda k, t_=t_: t_[:, k, tok] for t_ in (o_hi, o_lo)],
                                                 [lambda k, w_=w_: w_[:, w, k, :] for w_ in (w_hi, w_lo)])
                        last.then_inc(sem["made"], 1)

                    if kind in ("gate", "up"):
                        pe.wait_ge(sem["drained_dve"], tally.after(("transpose", "x2", what), "drained_dve"))
                        for k in range(DK):
                            for part in (t_hi, t_lo):
                                last = nc.tensor.matmul(bank[:, 0:SEQ], gate_up[:, int(kind == "up"), k, n * P:(n + 1) * P],
                                                        part[:, k, what * SEQ:(what + 1) * SEQ],
                                                        start=(k == 0 and part is t_hi), stop=(k == DK - 1 and part is t_lo))
                        last.then_inc(sem["made"], 1)

                    if kind == "down":
                        pe.wait_ge(sem["hidden"], tally.after(("split", n, HK - 1), "hidden"))
                        for m in range(2):
                            tok = slice((2 * n + m) * P, (2 * n + m + 1) * P)
                            for k in range(HK):
                                for part in (h_hi, h_lo):
                                    last = nc.tensor.matmul(bank[:, m * D:(m + 1) * D], part[:, k, tok], down_w[:, k, :],
                                                            start=(k == 0 and part is h_hi), stop=(k == HK - 1 and part is h_lo))
                        last.then_inc(sem["made"], 1)
                    if kind == "exps":
                        probs_slot[what, n] = tally.local["exps"] % PROBS
                    tally.passed(step)
            probs_slot = {}
            tables(pe, tally, walk)

        @block.scalar
        def _(act):
            act.wait_ge(arrived["queries_keys"], 16)
            for w in range(2):
                part = slice(w * WCOLS, (w + 1) * WCOLS)
                nc.scalar.copy(w_hi2[:, part], stage_self[:, part]).then_inc(first_hi, 1)
            act.wait_ge(arrived["small"], 32)
            tally = Tally()

            def walk(steps, front, back):
                for step in steps:
                    kind, what, n = step
                    bank = general[:, tally.bank(), :]
                    if kind in ("transpose", "project", "turn"):
                        act.wait_ge(sem["made"], tally.now("made") + 1)
                        if kind == "turn":
                            nc.scalar.activation(o_hi[:].rearrange("p k t -> p (k t)"), bank, ACT.Identity).then_inc(sem["high"], 1)
                        elif kind == "transpose":
                            dst, src = turned(t_hi, bank, what, n)
                            nc.scalar.activation(dst, src, ACT.Identity).then_inc(sem["high"], 1)
                        else:
                            nc.scalar.activation(p_hi[:, n, :], bank, ACT.Identity,
                                                 bias=feature_bias(what, n)).then_inc(sem["high"], 1)
                    if kind == "stack" and drained_by(step) == "act":
                        act.wait_ge(sem["made"], tally.now("made") + 1)
                        nc.scalar.activation(stacks[what][:, n, :], bank, ACT.Identity,
                                             bias=b_qk[:, 4:5] if what[1] == "k" else 0.0).then_inc(sem["drained_act"], 1)
                    if (kind, what) == ("value", "sv"):
                        act.wait_ge(sem["made"], tally.now("made") + 1)
                        nc.scalar.copy(values["sv"][:, 2 * n:2 * n + 2, :, 0:HD],
                                       bank.rearrange("p (t h d) -> p t h d", t=2, h=HEADS)).then_inc(sem["drained_act"], 1)
                    if kind == "exps":
                        width = 2 * SEQ if what[0] == "c" else SEQ + P
                        act.wait_ge(sem["logits"], tally.now("logits") + 1)
                        nc.scalar.activation(probs[:, tally.local["exps"] % PROBS, 0:width], logit[:, tally.slot("logits"), 0:width], ACT.Exp,
                                             scale=CROSS_SCALE if what[0] == "c" else SELF_SCALE).then_inc(sem["exps"], 1)
                    if kind == "weigh":
                        act.wait_ge(sem["summed"], tally.now("summed") + 1)
                        nc.scalar.copy(o_un[:, n, :], summed[:, n % 2, :]).then_inc(sem["unweighed"], 1)
                    if kind == "gate":
                        act.wait_ge(sem["made"], tally.now("made") + 1)
                        nc.scalar.activation(tanh[:, n % 2, 0:SEQ], bank[:, 0:SEQ], ACT.Tanh, scale=0.5 * QSCALE).then_inc(sem["high"], 1)
                    if kind == "split":
                        act.wait_ge(sem["drained_dve"], tally.after(("up", what, n), "drained_dve"))
                        nc.scalar.copy(h_hi[:, n, what * SEQ:(what + 1) * SEQ], hidden[:, n % 2, 0:SEQ]).then_inc(sem["hidden_high"], 1)
                    tally.passed(step)
            tables(act, tally, walk)

        @block.vector
        def _(dve):
            for w in range(2):
                part = slice(w * WCOLS, (w + 1) * WCOLS)
                dve.wait_ge(first_hi, w + 1)
                nc.vector.tensor_tensor(w_lo2[:, part], stage_self[:, part], w_hi2[:, part].bitcast(f32), ALU.subtract)
            nc.vector.memset(values["sv"][:, :, :, HD + 1:VW], 0.0)
            nc.vector.memset(values["sv"][:, :, :, HD:HD + 1], 1.0)
            dve.wait_ge(arrived["tables"], 32)
            nc.vector.tensor_copy(select[:], stage_tables[:, P:])
            nc.vector.tensor_copy(causal[:], stage_tables[:, 0:P])
            dve.wait_ge(arrived["small"], 32)
            nc.vector.tensor_copy(ident_bf[:], ident[:]).then_inc(prepared, 1)
            dve.wait_ge(arrived["bias_vo"], 16)
            tally = Tally()

            def own(ins):
                own_done[0] += 1
                ins.then_inc(sem["dve_own"], 1)
                dve.wait_ge(sem["dve_own"], tally.now("dve_own") + own_done[0])
            own_done = [0]

            def normalise_stats(rows, which, first):
                for m in range(2):
                    last = nc.vector.bn_stats(bn[:, m, :], rows[:, first + m, :])
                    if m == 1:
                        own(last)
                        apart(dve)
                for m in range(2):
                    last = nc.vector.bn_aggr(norms[which][:, first + m, :], bn[:, m, :])
                    last.then_inc(sem["stats"], 1)

            def walk(steps, front, back):
                for step in steps:
                    kind, what, n = step
                    own_done[0] = 0
                    bank = general[:, tally.bank(), :]
                    mine = "drained_dve" in signals(step)
                    if mine and kind != "maxima":
                        dve.wait_ge(sem["made"], tally.now("made") + 1)
                    if kind in ("transpose", "project", "turn"):
                        dve.wait_ge(sem["high"], tally.now("high") + 1)
                        if kind == "turn":
                            nc.vector.tensor_tensor(o_lo[:].rearrange("p k t -> p (k t)"), bank,
                                                    o_hi[:].rearrange("p k t -> p (k t)").bitcast(f32), ALU.subtract).then_inc(sem["drained_dve"], 1)
                        elif kind == "transpose":
                            (dst, src), (high, _) = (turned(t, bank, what, n) for t in (t_lo, t_hi))
                            nc.vector.tensor_tensor(dst, src, high.bitcast(f32), ALU.subtract).then_inc(sem["drained_dve"], 1)
                        else:
                            nc.vector.scalar_tensor_tensor(out=p_lo[:, n, :], in0=bank, scalar=feature_bias(what, n),
                                                           in1=p_hi[:, n, :].bitcast(f32), op0=ALU.add,
                                                           op1=ALU.subtract).then_inc(sem["drained_dve"], 1)
                    if kind == "stack" and mine:
                        if what[1] == "k":
                            ins = nc.vector.tensor_scalar(stacks[what][:, n, :], bank, b_qk[:, 4:5], None, ALU.add)
                        else:
                            ins = nc.vector.tensor_copy(stacks[what][:, n, :], bank)
                        ins.then_inc(sem["drained_dve"], 1)
                    if (kind, what) == ("value", "cv"):
                        nc.vector.tensor_tensor(values["cv"][:, 2 * n:2 * n + 2, :, 0:HD],
                                                bank.rearrange("p (t h d) -> p t h d", t=2, h=HEADS),
                                                b_vo[:, 0, :].rearrange("p (h d) -> p h d", h=HEADS).unsqueeze(1).broadcast_to([P, 2, HEADS, HD]),
                                                ALU.add).then_inc(sem["drained_dve"], 1)
                    if kind == "scores":
                        dve.wait_ge(sem["scores"], tally.now("scores") + 1)
                        bank, at, par = score[:, tally.slot("scores"), :], head_index(n), STAGES[what] % 2
                        if what[0] == "c":
                            nc.vector.tensor_reduce(neg_max[:, par, :, at], bank.rearrange("p (t k) -> p t k", t=2), AX, ALU.max,
                                                    negate=True).then_inc(sem["row_max"], 1)
                        else:
                            nc.vector.tensor_reduce(row_max[:, par, :, at], bank[:, 0:3 * P].rearrange("p (t k) -> p t k", t=3), AX,
                                                    ALU.max, negate=True).then_inc(sem["row_max"], 1)
                    if kind == "gather":
                        par = STAGES[what] % 2
                        dve.wait_ge(sem["row_max"], tally.after(("scores", what, HEADS - 1), "row_max"))
                        nc.vector.tensor_copy(neg_max[:, par, 0, :], row_max[:, par, 0, :]).then_inc(sem["neg_max"], 1)
                        nc.vector.tensor_tensor(neg_max[:, par, 1, :], row_max[:, par, 1, :], row_max[:, par, 2, :],
                                                ALU.min).then_inc(sem["neg_max"], 1)
                    if kind == "maxima":
                        dve.wait_ge(sem["made"], tally.now("made") + 1)
                        wait_for(dve, sem["max_sent"], tally.now("max_sent"))
                        nc.vector.tensor_copy(max_t[:], bank[0:HEADS, 0:SEQ]).then_inc(sem["drained_dve"], 1)
                    if kind == "normalise":
                        heads = bank.rearrange("p (h c) -> p h c", c=VW)
                        own(nc.vector.reciprocal(inv[:, n, :], heads[:, :, HD]))
                        nc.vector.tensor_tensor(o_tok[:, n, :].rearrange("p (h d) -> p h d", d=HD), heads[:, :, 0:HD],
                                                inv[:, n, :].unsqueeze(2).broadcast_to([P, HEADS, HD]), ALU.mult).then_inc(sem["drained_dve"], 1)
                    if kind == "output":
                        b = int(what[1])
                        rows = r1 if what[0] == "s" else r2
                        res = "residual_x" if what[0] == "s" else "residual_x1"
                        dve.wait_ge(sem[res], tally.now(res))
                        ins = nc.vector.tensor_tensor(rows[:, 2 * b:2 * b + 2, :], bank.rearrange("p (t d) -> p t d", t=2),
                                                      rows[:, 2 * b:2 * b + 2, :], ALU.add)
                        ins.then_inc(sem["drained_dve"], 1)
                    if kind == "gate":
                        if (what, n) != (0, 0):
                            dve.wait_ge(sem["drained_dve"], tally.after(("up",) + before(what, n, 1), "drained_dve"))
                        dve.wait_ge(sem["high"], tally.now("high") + 1)
                        nc.vector.scalar_tensor_tensor(out=gated[:, 0:SEQ], in0=tanh[:, n % 2, 0:SEQ], scalar=1.0, in1=bank[:, 0:SEQ],
                                                       op0=ALU.add, op1=ALU.mult).then_inc(sem["drained_dve"], 1)
                    if kind == "up":
                        dve.wait_ge(sem["drained_dve"], tally.after(("gate", what, n), "drained_dve"))
                        if (what, n) > (0, 1):
                            dve.wait_ge(sem["hidden"], tally.after(("split",) + before(what, n, 2), "hidden"))
                        nc.vector.tensor_tensor(hidden[:, n % 2, 0:SEQ], gated[:, 0:SEQ], bank[:, 0:SEQ], ALU.mult).then_inc(sem["drained_dve"], 1)
                    if kind == "split":
                        cols = slice(what * SEQ, (what + 1) * SEQ)
                        dve.wait_ge(sem["hidden_high"], tally.now("hidden_high") + 1)
                        nc.vector.tensor_tensor(h_lo[:, n, cols], hidden[:, n % 2, 0:SEQ], h_hi[:, n, cols].bitcast(f32),
                                                ALU.subtract).then_inc(sem["hidden"], 1)
                    if kind == "down":
                        rows = r2[:, 2 * n:2 * n + 2, :]
                        nc.vector.scalar_tensor_tensor(out=rows, in0=bank.rearrange("p (t d) -> p t d", t=2), scalar=0.5 * QSCALE ** 3,
                                                       in1=rows, op0=ALU.mult, op1=ALU.add).then_inc(sem["drained_dve"], 1)
                    if kind == "stats":
                        rows, which = {"s": (r1, "x1"), "c": (r2, "x2"), "y": (r2, "y")}[what[0]]
                        summed_up = ("down", "", int(what[1])) if what[0] == "y" else ("output", what, 0)
                        dve.wait_ge(sem["drained_dve"], tally.after(summed_up, "drained_dve"))
                        normalise_stats(rows, which, 2 * int(what[1]))
                    if kind == "norm":
                        dst, rows, which = {"s": (x1, r1, "x1"), "c": (r2, r2, "x2"), "y": (r2, r2, "y")}[what[0]]
                        dve.wait_ge(sem["rstd"], tally.after(("stats", what, 0), "rstd"))
                        if back is None and step == ("norm", "s0", 0):
                            dve.wait_ge(pool_ready, 3)
                        for t in range(2 * int(what[1]), 2 * int(what[1]) + 2):
                            nc.vector.tensor_scalar(dst[:, t, :], rows[:, t, :], norms[which][:, t, 0:1], rstds[which][:, t:t + 1],
                                                    ALU.subtract, ALU.mult).then_inc(sem[which], 1)
                    tally.passed(step)
            tables(dve, tally, walk, vector_order)

        @block.gpsimd
        def _(pool):
            nc.gpsimd.memset(half[:], -0.5)
            lots = [(arrived["values_out"], stage_self[:, 2 * WCOLS:3 * WCOLS], slice(2 * WCOLS, 3 * WCOLS), pool_ready),
                    (arrived["values_out"], stage_self[:, 3 * WCOLS:], slice(3 * WCOLS, 4 * WCOLS), pool_ready),
                    (arrived["later0"], flat(x1), slice(4 * WCOLS, 6 * WCOLS), cross_read),
                    (arrived["later1"], flat(r2), slice(6 * WCOLS, 8 * WCOLS), cross_read)]
            for n, (arrival, src, part, done) in enumerate(lots):
                pool.wait_ge(arrival, 16)
                nc.gpsimd.tensor_copy(w_hi2[:, part], src).then_inc(later_hi, 1)
                pool.wait_ge(later_hi, n + 1)
                nc.gpsimd.tensor_tensor(w_lo2[:, part], src, w_hi2[:, part].bitcast(f32), ALU.subtract).then_inc(done, 1)
            pool.wait_ge(prepared, 1)
            nc.gpsimd.memset(values["cv"][:, :, :, HD + 1:VW], 0.0)
            nc.gpsimd.memset(values["cv"][:, :, :, HD:HD + 1], 1.0)
            for n, (lot, _, dst) in enumerate(LATER):
                if n >= 2:
                    pool.wait_ge(arrived[f"later{n}"], 16)
                    last = nc.gpsimd.tensor_copy(dst, lot.bitcast(i32))
            last.then_inc(pool_ready, 1)
            tally = Tally()

            def own(ins):
                own_done[0] += 1
                ins.then_inc(sem["pool_own"], 1)
                pool.wait_ge(sem["pool_own"], tally.now("pool_own") + own_done[0])
                apart(pool)
            own_done = [0]

            def inverse_deviation(which, first):
                pool.wait_ge(sem["stats"], tally.now("stats") + 2)
                apart(pool)
                v, two = ve[which], slice(first, first + 2)
                own(nc.gpsimd.tensor_scalar(v[:, two], norms[which][:, two, 1], EPS, None, ALU.add))
                nc.gpsimd.tensor_tensor(rstds[which][:, two], v[:, two], half[:], ALU.pow).then_inc(sem["rstd"], 1)

            def walk(steps, front, back):
                for step in steps:
                    kind, what, n = step
                    own_done[0] = 0
                    if (kind, n) == ("transpose", 0) and what == "x":
                        pool.wait_ge(sem["loaded_x"], tally.now("loaded_x") + 16)
                        wait_for(pool, sem["x1"], tally.now("x1"))
                        apart(pool)
                        nc.gpsimd.tensor_copy(r1[:], x_in[:]).then_inc(sem["residual_x"], 1)
                    if kind == "residual":
                        pool.wait_ge(sem["x1"], tally.now("x1"))
                        pool.wait_ge(sem["stored"], tally.now("stored") + 1)
                        apart(pool)
                        nc.gpsimd.tensor_tensor(r2[:], x1[:], b_vo[:, 1, :].unsqueeze(1).broadcast_to([P, TT, D]),
                                                ALU.add).then_inc(sem["residual_x1"], 1)
                    if kind == "exps" and what[0] == "s":
                        pool.wait_ge(sem["exps"], tally.now("exps") + 1)
                        apart(pool)
                        blocks = probs[:, tally.local["exps"] % PROBS, :].rearrange("p (a b) -> p a b", a=2)[:, :, 0:P]
                        nc.gpsimd.affine_select(out=blocks, in_=blocks, compare_op=ALU.is_ge, fill=0.0, base=0,
                                                pattern=[[0, 2], [1, P]], channel_multiplier=-1).then_inc(sem["masked"], 1)
                    if kind == "stats":
                        inverse_deviation({"s": "x1", "c": "x2", "y": "y"}[what[0]], 2 * int(what[1]))
                    tally.passed(step)
            tables(pool, tally, walk)


def _constants():
    import numpy as np
    places = {("q", "hi"): (0, 1), ("q", "lo"): (2,), ("k", "hi"): (1, 2), ("k", "lo"): (0,)}
    sel = np.zeros((P, SELECTS), np.float32)
    for which, blocks in places.items():
        for head in range(P // HD):
            for d in range(HD):
                for blk in blocks:
                    sel[head * HD + d, SELECT_AT[which] + head // 2 * P + head % 2 * SLOT + blk * HD + d] = 1.0
    row = np.arange(P)
    mask = np.where(row[None, :] > row[:, None], MASKED, 0.0).astype(np.float32)
    one_row = (row % SLOT == MAX_ROW).astype(np.float32)[:, None]
    return sel, np.eye(P, dtype=np.float32), mask, one_row


def kernel(**inputs):
    import numpy as np
    import concourse.bacc as _bacc
    from concourse import mybir as _mybir
    from concourse.bass_utils import run_bass_kernel_spmd as _run

    a = {name: np.asarray(v) for name, v in inputs.items()}

    def rows(w):
        return w.reshape(-1, P, w.shape[1]).transpose(1, 0, 2)

    qkv = a["L0_attn_w_qkv"].reshape(D, HEADS, 3, HD).transpose(2, 0, 1, 3).reshape(3, D, D)
    mats = [qkv[0], qkv[1], qkv[2], a["L0_attn_w_o"]] + [a["L0_xattn_W" + n].T for n in "qkvo"]
    weights = np.stack([rows(m) for m in mats], 1).reshape(P, -1)
    gate_up = np.stack([rows(a["L0_ffn_w_gate"].T), rows(a["L0_ffn_w_up"].T)], 1).reshape(P, -1)
    down = rows(a["L0_ffn_w_down"].T).reshape(P, -1)
    sel, eye, mask, one_row = _constants()
    bias_qk = np.concatenate([a["L0_xattn_bq"].reshape(2, P).T, a["L0_xattn_bk"].reshape(2, P).T, one_row], 1)
    bias_vo = np.broadcast_to(np.stack([a["L0_xattn_bv"], a["L0_xattn_bo"]])[None], (P, 2, D))
    laid = {"x": a["x"].reshape(SEQS * SEQ, D), "ctx": a["ctx_1024"].reshape(SEQS * SEQ, D), "weights": weights,
            "gate_up": gate_up, "down": down, "bias_qk": bias_qk, "bias_vo": bias_vo, "selectors": sel, "ident": eye, "mask": mask}

    nc = _bacc.Bacc("TRN2", target_bir_lowering=False, num_devices=1)
    nc.disable_value_cache = True
    arrays, args = {}, []
    for name, value in laid.items():
        value = np.ascontiguousarray(value)
        arrays[name + "_dram"] = value
        args.append(nc.dram_tensor(name + "_dram", value.shape, _mybir.dt.from_np(value.dtype), kind="ExternalInput").ap())
    y = nc.dram_tensor("y_dram", (SEQS * SEQ, D), _mybir.dt.float32, kind="ExternalOutput").ap()
    decoder_layer(nc, *args, y)
    r = _run(nc, [arrays], core_ids=[0])
    return r.results[0]["y_dram"].reshape(SEQS, SEQ, D)
```
